# Optimizing a Trainium2 kernel written in Bass

```python
import numpy as np
import jax
import jax.numpy as jnp

def _softmax(x, axis=-1):
    return jax.nn.softmax(x, axis=axis)

def _gelu(x):
    return jax.nn.gelu(x, approximate=True)

def _silu(x):
    return jax.nn.silu(x)

def _sigmoid(x):
    return jax.nn.sigmoid(x)

def _layernorm(x, axis=-1, eps=1e-05):
    m = jnp.mean(x, axis=axis, keepdims=True)
    v = jnp.var(x, axis=axis, keepdims=True)
    return (x - m) / jnp.sqrt(v + eps)

def _scatter_add(tgt, idx, src, axis=0):
    return tgt.at[idx].add(src)

def _segment_sum(src, seg, n):
    return jax.ops.segment_sum(src, seg, n)
kernel_name = 'mk_cond_resid_d2_seqx_r8_fa2a04'

def setup_inputs(seed: int=0):
    np.random.seed(seed)
    _w = jnp.asarray

    def _rec_inputs():
        import jax
        import jax.numpy as jnp
        _rk = jax.random.key(seed)
        x = -7.109e-05 + 0.9999 * jax.random.normal(jax.random.fold_in(_rk, 1), (64, 32, 256), jnp.float32)
        _lenS = 32 - jax.random.randint(jax.random.fold_in(_rk, 7), (64,), 0, max(1, 32 // 4) + 1, jnp.int32)
        _lenS2 = 32 - jax.random.randint(jax.random.fold_in(_rk, 8), (64,), 0, max(1, 32 // 4) + 1, jnp.int32)
        itok_B_1_198 = jax.random.randint(jax.random.fold_in(_rk, 11), (64,), 1, 199, jnp.int32)
        itok_B_0_7 = jax.random.randint(jax.random.fold_in(_rk, 12), (64,), 0, 8, jnp.int32)
        return (x, itok_B_1_198, itok_B_0_7)
    x, itok_B_1_198, itok_B_0_7 = _rec_inputs()

    def _L0_cond_setup():
        import jax, jax.numpy as jnp
        import numpy as np
        B, C, T = (128, 32, 256)
        S, D = (200, 32)
        key = jax.random.key(seed)
        k1, k2, k3 = jax.random.split(key, 3)
        x = jax.random.normal(k1, (B, C, T), dtype=jnp.float32)
        conditions = jax.random.randint(k2, (B,), 0, S, dtype=jnp.int64)
        weights = jax.random.normal(k3, (S, C, D), dtype=jnp.float32) / jnp.sqrt(jnp.float32(C))
        return {'x': x, 'conditions': conditions, 'weights': weights}
    _L0_cond_all = _L0_cond_setup()
    _L0_cond_in = {k: v for k, v in _L0_cond_all.items() if k in ('weights',)}
    del _L0_cond_all

    def _L1_cond_setup():
        import jax, jax.numpy as jnp
        import numpy as np

        def _lora_linear(x, W, A, B, adapter_indices):
            base = jnp.einsum('bsd,df->bsf', x, W)
            Ai = A[adapter_indices]
            Bi = B[adapter_indices]
            lora = jnp.einsum('bsr,brf->bsf', jnp.einsum('bsd,bdr->bsr', x, Ai), Bi)
            return base + lora
        key = jax.random.key(seed)
        ks = jax.random.split(key, 10)
        H, I, N, R = (256, 1024, 8, 16)
        B, S = (4, 256)
        std_h = 1.0 / np.sqrt(H)
        std_i = 1.0 / np.sqrt(I)
        x = jax.random.normal(ks[0], (B, S, H), dtype=jnp.float32)
        adapter_indices = jax.random.randint(ks[1], (B,), 0, N, dtype=jnp.int32)
        Wg = jax.random.normal(ks[2], (H, I), dtype=jnp.float32) * std_h
        Wu = jax.random.normal(ks[3], (H, I), dtype=jnp.float32) * std_h
        Wd = jax.random.normal(ks[4], (I, H), dtype=jnp.float32) * std_i
        Ag = jax.random.normal(ks[5], (N, H, R), dtype=jnp.float32) * std_h
        Bg = jnp.zeros((N, R, I), dtype=jnp.float32) + 0.01
        Au = jax.random.normal(ks[6], (N, H, R), dtype=jnp.float32) * std_h
        Bu = jnp.zeros((N, R, I), dtype=jnp.float32) + 0.01
        Ad = jax.random.normal(ks[7], (N, I, R), dtype=jnp.float32) * std_i
        Bd = jnp.zeros((N, R, H), dtype=jnp.float32) + 0.01
        return {'x': x, 'Wg': Wg, 'Wu': Wu, 'Wd': Wd, 'Ag': Ag, 'Bg': Bg, 'Au': Au, 'Bu': Bu, 'Ad': Ad, 'Bd': Bd, 'adapter_indices': adapter_indices}
    _L1_cond_all = _L1_cond_setup()
    _L1_cond_in = {k: v for k, v in _L1_cond_all.items() if k in ('Wg', 'Wu', 'Wd', 'Ag', 'Bg', 'Au', 'Bu', 'Ad', 'Bd')}
    del _L1_cond_all
    return {'x': x, 'itok_B_1_198': itok_B_1_198, 'itok_B_0_7': itok_B_0_7, 'L0_cond_weights': _L0_cond_in['weights'], 'L1_cond_Wg': _L1_cond_in['Wg'], 'L1_cond_Wu': _L1_cond_in['Wu'], 'L1_cond_Wd': _L1_cond_in['Wd'], 'L1_cond_Ag': _L1_cond_in['Ag'], 'L1_cond_Bg': _L1_cond_in['Bg'], 'L1_cond_Au': _L1_cond_in['Au'], 'L1_cond_Bu': _L1_cond_in['Bu'], 'L1_cond_Ad': _L1_cond_in['Ad'], 'L1_cond_Bd': _L1_cond_in['Bd']}

def reference(x, itok_B_1_198, itok_B_0_7, L0_cond_weights, L1_cond_Wg, L1_cond_Wu, L1_cond_Wd, L1_cond_Ag, L1_cond_Bg, L1_cond_Au, L1_cond_Bu, L1_cond_Ad, L1_cond_Bd):
    import jax
    import jax.numpy as jnp

    def _L0_cond_ref(x, conditions, weights):
        import jax, jax.numpy as jnp
        import numpy as np
        B, C, T = (128, 32, 256)
        S, D = (200, 32)
        w = weights[conditions]
        return jnp.einsum('bct,bcd->bdt', x, w)

    def _L1_cond_ref(x, Wg, Wu, Wd, Ag, Bg, Au, Bu, Ad, Bd, adapter_indices):
        import jax, jax.numpy as jnp
        import numpy as np

        def _lora_linear(x, W, A, B, adapter_indices):
            base = jnp.einsum('bsd,df->bsf', x, W)
            Ai = A[adapter_indices]
            Bi = B[adapter_indices]
            lora = jnp.einsum('bsr,brf->bsf', jnp.einsum('bsd,bdr->bsr', x, Ai), Bi)
            return base + lora
        gate = _lora_linear(x, Wg, Ag, Bg, adapter_indices)
        up = _lora_linear(x, Wu, Au, Bu, adapter_indices)
        h = jax.nn.silu(gate) * up
        return _lora_linear(h, Wd, Ad, Bd, adapter_indices)
    x = x + _L0_cond_ref(x, itok_B_1_198, L0_cond_weights)
    x = x + _L1_cond_ref(x, L1_cond_Wg, L1_cond_Wu, L1_cond_Wd, L1_cond_Ag, L1_cond_Bg, L1_cond_Au, L1_cond_Bu, L1_cond_Ad, L1_cond_Bd, itok_B_0_7)
    return x

_drawn_inputs = setup_inputs


def setup_inputs(seed=0):
    import zlib

    import numpy as np

    out = dict(_drawn_inputs(seed))
    spreads = {'L1_cond_Bg': (0.009999999776482582, 0.2),
     'L1_cond_Bu': (0.009999999776482582, 0.2),
     'L1_cond_Bd': (0.009999999776482582, 0.2)}
    factors = {}
    for name, (base, spread) in spreads.items():
        noise = np.random.default_rng([zlib.crc32(name.encode()), seed]).standard_normal(out[name].shape)
        drawn = base * np.exp(spread * noise) if base else spread * noise
        out[name] = jnp.asarray(drawn.astype(out[name].dtype))
    for name, factor in factors.items():
        out[name] = (out[name] * factor).astype(out[name].dtype)
    return out
```

```python
from contextlib import ExitStack

import concourse.bass as bass
from concourse import mybir
from concourse.alu_op_type import AluOpType as ALU

F32 = mybir.dt.float32
F32R = mybir.dt.float32r
I32 = mybir.dt.int32
U32 = mybir.dt.uint32
ACT = mybir.ActivationFunctionType

HI, LO = 0, 1
PASSES = ((HI, HI), (HI, LO), (LO, HI))


def cond_lora_block(
    nc: bass.Bass,
    x: bass.AP,
    condition: bass.AP,
    adapter: bass.AP,
    w_cond: bass.AP,
    Wg: bass.AP,
    Wu: bass.AP,
    Wd: bass.AP,
    Ag: bass.AP,
    Bg: bass.AP,
    Au: bass.AP,
    Bu: bass.AP,
    Ad: bass.AP,
    Bd: bass.AP,
    out: bass.AP,
):
    B, C, H = x.shape
    S = w_cond.shape[0]
    I = Wg.shape[1]
    N, _, R = Ag.shape
    P = 128
    TB = P // C
    TILES = B * C // P
    GT = 4
    T = GT * P
    GROUPS = TILES // GT
    GB = GT * TB
    HK = H // P
    Q = I // P
    WCH = 4
    WC = I // WCH
    QC = Q // WCH
    NR = N * R
    assert NR == P and T == 512 and TB * C == P and H == 256
    AC = 2 * HK + Q
    A_ROWS = N * AC
    RB = R // 4

    tiles_of = lambda ap: ap.rearrange("b c t -> (b c) t").rearrange("(j p) t -> p j t", p=P)
    x_dram = tiles_of(x)
    out_dram = tiles_of(out)
    w_rows = w_cond.rearrange("s c d -> (s c) d")

    with ExitStack() as ctx:
        def sb(name, shape, dt):
            return ctx.enter_context(nc.sbuf_tensor(name, shape, dt))

        def sem(name):
            return ctx.enter_context(nc.semaphore(name))

        ident = sb("ident", [P, P], F32)
        ident_r = sb("ident_r", [P, P], F32R)
        eye_c = sb("eye_c", [P, C], F32)
        p_index = sb("p_index", [P, 1], F32)
        c_index = sb("c_index", [P, 1], F32)
        cond_bc = sb("cond_bc", [P, B], I32)
        adapter_bc = sb("adapter_bc", [P, B], I32)
        w_row_index = sb("w_row_index", [P, TILES], U32)
        mask_d = sb("mask_d", [P, B], F32)
        mask_ge = sb("mask_ge", [P, B], F32)
        mask = sb("mask", [P, B], F32)
        x_raw = sb("x_raw", [P, GT, H], F32)
        xs = [sb(f"x_{s}", [P, GT, H], F32R) for s in ("hi", "lo")]
        w_gathered = sb("w_gathered", [P, TILES, C], F32)
        w_plus_i = sb("w_plus_i", [P, GT, C], F32)
        mix = [sb(f"mix_{s}", [P, GT, P], F32R) for s in ("hi", "lo")]
        x1 = [sb(f"x1_{s}", [P, HK, T], F32R) for s in ("hi", "lo")]
        w_raw = [sb(f"w_raw_{m}", [P, HK, I], F32) for m in ("g", "u")]
        w_gu = [[sb(f"w_{m}_{s}", [P, HK, I], F32R) for s in ("hi", "lo")] for m in ("g", "u")]
        wd = [sb(f"wd_{s}", [P, Q, H], F32R) for s in ("hi", "lo")]
        a_rows = sb("a_rows", [A_ROWS, P, R], F32)
        a_t = [sb(f"a_t_{s}", [P, AC, N, R], F32R) for s in ("hi", "lo")]
        b_raw = sb("b_raw", [P, 2 * I + H], F32)
        b_all = [sb(f"b_{s}", [P, 2 * I + H], F32R) for s in ("hi", "lo")]
        z32 = sb("z32", [P, T], F32)
        z = [[sb(f"z_{m}_{s}", [P, T], F32R) for s in ("hi", "lo")] for m in ("g", "u")]
        zd = [sb(f"zd_{s}", [P, T], F32R) for s in ("hi", "lo")]
        h32 = sb("h32", [P, 2, T], F32)
        h = [sb(f"h_{s}", [P, Q, T], F32R) for s in ("hi", "lo")]
        out_sb = sb("out_sb", [P, GT, H], F32)

        bank = [ctx.enter_context(nc.psum_tensor(f"bank{i}", [P, 512], F32)) for i in range(8)]
        ps_gate, ps_up, ps_out, ps_misc = bank[0:2], bank[2:4], bank[4:6], bank[6:8]

        wd_raw = w_raw[0][:, :, :].rearrange("p k n -> p (k n)").rearrange("p (q n) -> p q n", q=Q)

        cond_in = sem("cond_in")
        adapter_in = sem("adapter_in")
        x_in = sem("x_in")
        a_in = sem("a_in")
        w_in = [sem(f"w_in{c}") for c in range(WCH)]
        b_in = sem("b_in")
        wd_in = sem("wd_in")
        gathered = [sem(f"gathered{g}") for g in range(GROUPS)]
        consts_ready = sem("consts_ready")
        index_const_ready = sem("index_const_ready")
        ident_memset = sem("ident_memset")
        index_ready = sem("index_ready")
        eye_ready = sem("eye_ready")
        mix_zeroed = sem("mix_zeroed")
        mask_step = sem("mask_step")
        mask_ready = sem("mask_ready")
        ident_r_ready = sem("ident_r_ready")
        x_hi_ready = sem("x_hi_ready")
        x_lo_ready = sem("x_lo_ready")
        w_plus_i_ready = sem("w_plus_i_ready")
        mix_hi_ready = sem("mix_hi_ready")
        mix_ready = sem("mix_ready")
        a_turned = sem("a_turned")
        a_hi_ready = sem("a_hi_ready")
        a_ready = sem("a_ready")
        w_hi_ready = sem("w_hi_ready")
        w_ready = sem("w_ready")
        b_hi_ready = sem("b_hi_ready")
        b_ready = sem("b_ready")
        wd_hi_ready = sem("wd_hi_ready")
        wd_ready = sem("wd_ready")
        mixed = sem("mixed")
        x1_hi_ready = sem("x1_hi_ready")
        x1_ready = sem("x1_ready")
        z_done = sem("z_done")
        z_masked = sem("z_masked")
        z_hi_ready = sem("z_hi_ready")
        z_ready = sem("z_ready")
        gate_up_done = sem("gate_up_done")
        silu_done = sem("silu_done")
        h_done = sem("h_done")
        h_hi_ready = sem("h_hi_ready")
        h_ready = sem("h_ready")
        residual_done = sem("residual_done")
        zd_done = sem("zd_done")
        zd_masked = sem("zd_masked")
        zd_hi_ready = sem("zd_hi_ready")
        zd_ready = sem("zd_ready")
        out_done = sem("out_done")
        out_copied = sem("out_copied")
        out_stored = [sem(f"out_stored{b}") for b in range(2)]

        block = ctx.enter_context(nc.Block())

        def group_mask(g):
            return mask[:, bass.ds(g * GB, GB)].unsqueeze(2).to_broadcast([P, GB, C])

        def by_batch(ap):
            return ap.rearrange("p (b c) -> p b c", c=C)

        def a_source(b, first, n_chunks):
            v = bank[b][:, :].rearrange("p (r e) -> p r e", r=4)
            return v[:, :, first:first + N * n_chunks].rearrange("p r (n c) -> p n c r", n=N)

        def a_place(s, b, first, n_chunks):
            v = a_t[s][:, first:first + n_chunks, :, 4 * b:4 * b + 4]
            return v.rearrange("p c n r -> p n c r")

        A_PARTS = [(0, 0, HK), (N * HK, HK, HK), (2 * N * HK, 2 * HK, Q)]

        @block.sync
        def _(sp):
            sp.dma_start(cond_bc[:, :], condition.partition_broadcast(P)).then_inc(cond_in, 16)
            sp.dma_start(x_raw[:, :, :], x_dram[:, 0:GT, :]).then_inc(x_in, 16)
            for (row, _, k), A in zip(A_PARTS, (Ag, Au, Ad)):
                sp.dma_start(a_rows[row:row + N * k, :, :],
                             A.rearrange("n t r -> (n t) r").rearrange("(e p) r -> e p r", p=P)
                             ).then_inc(a_in, 16)
            for c in range(WCH):
                for m, W in enumerate((Wg, Wu)):
                    sp.dma_start(w_raw[m][:, :, c * WC:(c + 1) * WC],
                                 W.rearrange("(k p) n -> p k n", p=P)[:, :, c * WC:(c + 1) * WC]
                                 ).then_inc(w_in[c], 16)
            sp.wait_ge(w_ready, 2 * WCH)
            sp.dma_start(wd_raw, Wd.rearrange("(q p) n -> p q n", p=P)).then_inc(wd_in, 16)

            def store(g):
                for b in range(2):
                    sp.wait_ge(out_copied, 2 * g + b + 1)
                    sp.dma_start(out_dram[:, bass.ds(g * GT + 2 * b, 2), :],
                                 out_sb[:, 2 * b:2 * b + 2, :]).then_inc(out_stored[b], 16)

            def load_x(g):
                tile = g * GT
                sp.wait_ge(x_hi_ready, g)
                sp.wait_ge(x_lo_ready, g)
                sp.dma_start(x_raw[:, :, :], x_dram[:, bass.ds(tile, GT), :]).then_inc(x_in, 16)

            load_x(1)
            with sp.Fori(2, GROUPS) as ahead:
                store(ahead - 2)
                for b in range(2):
                    sp.wait_ge(out_stored[b], 16 * ahead - 16)
                load_x(ahead)
            store(GROUPS - 2)
            store(GROUPS - 1)
            for b in range(2):
                sp.wait_ge(out_stored[b], 16 * GROUPS)

        @block.gpsimd
        def _(pool):
            nc.gpsimd.iota(p_index[:, :], [[0, 1]], base=0, channel_multiplier=1,
                           allow_small_or_imprecise_dtypes=True).then_inc(index_const_ready, 1)
            for q in range(TB):
                pool.wait_ge(index_const_ready, q + 1)
                nc.gpsimd.iota(c_index[q * C:(q + 1) * C, :], [[0, 1]], base=0, channel_multiplier=1,
                               allow_small_or_imprecise_dtypes=True).then_inc(index_const_ready, 1)
            pool.wait_ge(index_const_ready, 1 + TB)
            nc.gpsimd.memset(ident[:, :], 0.0).then_inc(ident_memset, 1)
            pool.wait_ge(ident_memset, 1)
            nc.gpsimd.affine_select(out=ident[:, :], in_=ident[:, :], compare_op=ALU.not_equal, fill=1.0,
                                    base=0, pattern=[[-1, P]], channel_multiplier=1
                                    ).then_inc(consts_ready, 1)
            pool.wait_ge(index_ready, TB)
            for j in range(TILES):
                nc.gpsimd.indirect_dma_start(
                    w_gathered[:, j, :], None, w_rows,
                    bass.IndirectOffsetOnAxis(ap=w_row_index[:, j:j + 1], axis=0),
                ).then_inc(gathered[j // GT], 16)
                if j == GT - 1:
                    pool.wait_ge(x_hi_ready, 1)
                    nc.gpsimd.tensor_tensor(xs[LO][:, :, :], x_raw[:, :, :], xs[HI][:, :, :].bitcast(F32),
                                            ALU.subtract).then_inc(x_lo_ready, 1)

            def z_lo(g):
                for m in range(2):
                    pool.wait_ge(z_hi_ready, 2 * g + m + 1)
                    nc.gpsimd.tensor_tensor(z[m][LO][:, :], z32[:, :], z[m][HI][:, :].bitcast(F32),
                                            ALU.subtract).then_inc(z_ready, 1)

            for m in range(2):
                pool.wait_ge(b_hi_ready, m + 1)
                nc.gpsimd.tensor_tensor(b_all[LO][:, m * I:(m + 1) * I], b_raw[:, m * I:(m + 1) * I],
                                        b_all[HI][:, m * I:(m + 1) * I].bitcast(F32),
                                        ALU.subtract).then_inc(b_ready, 1)
            z_lo(0)
            pool.wait_ge(b_hi_ready, 3)
            nc.gpsimd.tensor_tensor(b_all[LO][:, 2 * I:], b_raw[:, 2 * I:],
                                    b_all[HI][:, 2 * I:].bitcast(F32), ALU.subtract).then_inc(b_ready, 1)

            def group(g, more):
                for i in range(Q):
                    pool.wait_ge(h_hi_ready, Q * g + i + 1)
                    nc.gpsimd.tensor_tensor(h[LO][:, i, :], h32[:, i % 2, :], h[HI][:, i, :].bitcast(F32),
                                            ALU.subtract).then_inc(h_ready, 1)
                    if more and i == 4:
                        pool.wait_ge(x_hi_ready, g + 2)
                        nc.gpsimd.tensor_tensor(xs[LO][:, :, :], x_raw[:, :, :],
                                                xs[HI][:, :, :].bitcast(F32),
                                                ALU.subtract).then_inc(x_lo_ready, 1)
                pool.wait_ge(zd_hi_ready, g + 1)
                nc.gpsimd.tensor_tensor(zd[LO][:, :], z32[:, :], zd[HI][:, :].bitcast(F32),
                                        ALU.subtract).then_inc(zd_ready, 1)
                if more:
                    z_lo(g + 1)

            with pool.Fori(0, GROUPS - 1) as g:
                group(g, True)
            group(GROUPS - 1, False)

        @block.scalar
        def _(act):
            act.dma_start(adapter_bc[:, :], adapter.partition_broadcast(P)).then_inc(adapter_in, 16)
            for m, Bm in enumerate((Bg, Bu, Bd)):
                act.dma_start(b_raw[:, m * I:m * I + Bm.shape[2]],
                              Bm.rearrange("n r i -> (n r) i")).then_inc(b_in, 16)

            def x_hi(g):
                act.wait_ge(x_in, 16 * g + 16)
                nc.scalar.copy(xs[HI][:, :, :], x_raw[:, :, :]).then_inc(x_hi_ready, 1)

            def x1_hi(g):
                for k in range(HK):
                    act.wait_ge(mixed, HK * g + k + 1)
                    nc.scalar.copy(x1[HI][:, k, :], ps_misc[k][:, :]).then_inc(x1_hi_ready, 1)

            def z_hi(g):
                for m in range(2):
                    act.wait_ge(z_masked, 2 * g + m + 1)
                    nc.scalar.copy(z[m][HI][:, :], z32[:, :]).then_inc(z_hi_ready, 1)

            def w_hi(c):
                act.wait_ge(w_in[c], 32)
                for m in range(2):
                    nc.scalar.copy(w_gu[m][HI][:, :, c * WC:(c + 1) * WC],
                                   w_raw[m][:, :, c * WC:(c + 1) * WC]).then_inc(w_hi_ready, 1)

            x_hi(0)
            for b in range(RB):
                act.wait_ge(a_turned, b + 1)
                for row, chunk, k in A_PARTS:
                    nc.scalar.copy(a_place(HI, b, chunk, k), a_source(b, row, k)).then_inc(a_hi_ready, 1)
            x1_hi(0)
            w_hi(0)
            act.wait_ge(b_in, 48)
            for m in range(2):
                nc.scalar.copy(b_all[HI][:, m * I:(m + 1) * I],
                               b_raw[:, m * I:(m + 1) * I]).then_inc(b_hi_ready, 1)
            z_hi(0)
            for c in range(1, WCH):
                w_hi(c)
            nc.scalar.copy(b_all[HI][:, 2 * I:], b_raw[:, 2 * I:]).then_inc(b_hi_ready, 1)
            act.wait_ge(wd_in, 16)
            nc.scalar.copy(wd[HI][:, :, :], wd_raw).then_inc(wd_hi_ready, 1)

            def group(g, more):
                for i in range(Q):
                    act.wait_ge(gate_up_done, Q * g + i + 1)
                    if i >= 2:
                        act.wait_ge(h_ready, Q * g + i - 1)
                    nc.scalar.activation(h32[:, i % 2, :], ps_gate[i % 2][:, :], ACT.Silu
                                         ).then_inc(silu_done, 1)
                    if more and i == 3:
                        x_hi(g + 1)
                    act.wait_ge(h_done, Q * g + i + 1)
                    nc.scalar.copy(h[HI][:, i, :], h32[:, i % 2, :]).then_inc(h_hi_ready, 1)
                if more:
                    x1_hi(g + 1)
                act.wait_ge(zd_masked, g + 1)
                nc.scalar.copy(zd[HI][:, :], z32[:, :]).then_inc(zd_hi_ready, 1)
                if more:
                    z_hi(g + 1)

            with act.Fori(0, GROUPS - 1) as g:
                group(g, True)
            group(GROUPS - 1, False)

        @block.vector
        def _(dve):
            for s in (HI, LO):
                nc.vector.memset(mix[s][:, :, :].bitcast(F32), 0.0).then_inc(mix_zeroed, 1)
            dve.wait_ge(index_const_ready, 1 + TB)
            dve.wait_ge(cond_in, 16)
            for q in range(TB):
                at = slice(q * C, (q + 1) * C)
                nc.vector.tensor_scalar(w_row_index[at, :], cond_bc[at, q::TB], float(C), c_index[at, :],
                                        ALU.mult, ALU.add).then_inc(index_ready, 1)
            dve.wait_ge(consts_ready, 1)
            for q in range(TB):
                at = slice(q * C, (q + 1) * C)
                nc.vector.tensor_copy(eye_c[at, :], ident[at, at]).then_inc(eye_ready, 1)
            nc.vector.tensor_copy(ident_r[:, :], ident[:, :]).then_inc(ident_r_ready, 1)
            dve.wait_ge(adapter_in, 16)
            nc.vector.tensor_scalar(mask_d[:, :], adapter_bc[:, :], -float(R), p_index[:, :],
                                    ALU.mult, ALU.add).then_inc(mask_step, 1)
            dve.wait_ge(mask_step, 1)
            nc.vector.tensor_scalar(mask_ge[:, :], mask_d[:, :], 0.0, None, ALU.is_ge).then_inc(mask_step, 1)
            dve.wait_ge(mask_step, 2)
            nc.vector.scalar_tensor_tensor(mask[:, :], mask_d[:, :], R - 0.5, mask_ge[:, :],
                                           ALU.is_lt, ALU.mult).then_inc(mask_ready, 1)

            def mix_parts(g):
                nc.vector.tensor_tensor(w_plus_i[:, :, :], w_gathered[:, bass.ds(g * GT, GT), :],
                                        eye_c[:, :].unsqueeze(1).to_broadcast([P, GT, C]),
                                        ALU.add).then_inc(w_plus_i_ready, 1)
                dve.wait_ge(w_plus_i_ready, g + 1)
                for q in range(TB):
                    at = slice(q * C, (q + 1) * C)
                    nc.vector.tensor_copy(mix[HI][at, :, at], w_plus_i[at, :, :]).then_inc(mix_hi_ready, 1)
                dve.wait_ge(mix_hi_ready, TB * g + TB)
                for q in range(TB):
                    at = slice(q * C, (q + 1) * C)
                    nc.vector.tensor_tensor(mix[LO][at, :, at], w_plus_i[at, :, :],
                                            mix[HI][at, :, at].bitcast(F32),
                                            ALU.subtract).then_inc(mix_ready, 1)

            def x1_lo(g):
                for k in range(HK):
                    dve.wait_ge(x1_hi_ready, HK * g + k + 1)
                    nc.vector.tensor_tensor(x1[LO][:, k, :], ps_misc[k][:, :], x1[HI][:, k, :].bitcast(F32),
                                            ALU.subtract).then_inc(x1_ready, 1)

            def z_mask(g, first):
                for m in range(2):
                    dve.wait_ge(z_done, 2 * g + m + 1)
                    if m == 1:
                        dve.wait_ge(z_ready, 2 * g + 1)
                    elif not first:
                        dve.wait_ge(zd_ready, g)
                    nc.vector.tensor_tensor(by_batch(z32[:, :]), by_batch(ps_misc[m][:, :]), group_mask(g),
                                            ALU.mult).then_inc(z_masked, 1)

            def w_lo(c):
                for m in range(2):
                    dve.wait_ge(w_hi_ready, 2 * c + m + 1)
                    nc.vector.tensor_tensor(w_gu[m][LO][:, :, c * WC:(c + 1) * WC],
                                            w_raw[m][:, :, c * WC:(c + 1) * WC],
                                            w_gu[m][HI][:, :, c * WC:(c + 1) * WC].bitcast(F32),
                                            ALU.subtract).then_inc(w_ready, 1)

            dve.wait_ge(mix_zeroed, 2)
            dve.wait_ge(eye_ready, TB)
            dve.wait_ge(gathered[0], 16 * GT)
            mix_parts(0)
            for b in range(RB):
                dve.wait_ge(a_hi_ready, len(A_PARTS) * (b + 1))
                for row, chunk, k in A_PARTS:
                    nc.vector.tensor_tensor(a_place(LO, b, chunk, k), a_source(b, row, k),
                                            a_place(HI, b, chunk, k).bitcast(F32),
                                            ALU.subtract).then_inc(a_ready, 1)
            x1_lo(0)
            w_lo(0)
            dve.wait_ge(mask_ready, 1)
            z_mask(0, True)
            for c in range(1, WCH):
                w_lo(c)
            dve.wait_ge(wd_hi_ready, 1)
            nc.vector.tensor_tensor(wd[LO][:, :, :], wd_raw, wd[HI][:, :, :].bitcast(F32),
                                    ALU.subtract).then_inc(wd_ready, 1)
            for g in range(1, GROUPS):
                dve.wait_ge(gathered[g], 16 * GT)

            def group(g, more):
                for i in range(Q):
                    dve.wait_ge(silu_done, Q * g + i + 1)
                    nc.vector.tensor_tensor(h32[:, i % 2, :], h32[:, i % 2, :], ps_up[i % 2][:, :],
                                            ALU.mult).then_inc(h_done, 1)
                    if more and i == 2:
                        dve.wait_ge(mixed, HK * g + HK)
                        mix_parts(g + 1)
                if more:
                    x1_lo(g + 1)
                dve.wait_ge(zd_done, g + 1)
                nc.vector.tensor_tensor(by_batch(z32[:, :]), by_batch(ps_gate[0][:, :]), group_mask(g),
                                        ALU.mult).then_inc(zd_masked, 1)
                if more:
                    z_mask(g + 1, False)
                for b in range(2):
                    dve.wait_ge(out_done, 2 * g + b + 1)
                    if not more:
                        dve.wait_ge(out_stored[b], 16 * g)
                    nc.vector.tensor_copy(out_sb[:, 2 * b:2 * b + 2, :].rearrange("p j t -> p (j t)"),
                                          ps_out[b][:, :]).then_inc(out_copied, 1)

            with dve.Fori(0, GROUPS - 1) as g:
                group(g, True)
            group(GROUPS - 1, False)

        @block.tensor
        def _(pe):
            pe.wait_ge(consts_ready, 1)
            pe.wait_ge(a_in, 48)
            for r in range(R):
                at = slice((r % 4) * P, (r % 4) * P + A_ROWS)
                last = nc.tensor.transpose(bank[r // 4][:, at], a_rows[:, :, r], ident[0:A_ROWS, 0:A_ROWS])
                if r % 4 == 3:
                    last.then_inc(a_turned, 1)

            def mm(o, lhsT, rhs, start, stop):
                return nc.tensor.matmul(o, lhsT, rhs, start=start, stop=stop, skip_group_check=True)

            def x1_half(g, k):
                for j in range(GT):
                    for n, (a, b) in enumerate(PASSES):
                        last = mm(ps_misc[k][:, j * P:(j + 1) * P], xs[a][:, j, k * P:(k + 1) * P],
                                  mix[b][:, j, :], j == 0 and n == 0, j == GT - 1 and n == 2)
                last.then_inc(mixed, 1)

            def mix_group(g):
                pe.wait_ge(x_lo_ready, g + 1)
                pe.wait_ge(mix_ready, TB * g + TB)
                for k in range(HK):
                    x1_half(g, k)

            def z_gate_up(g):
                pe.wait_ge(x1_ready, HK * g + HK)
                for m in range(2):
                    for k in range(HK):
                        for n, (a, b) in enumerate(PASSES):
                            last = mm(ps_misc[m][:, :],
                                      a_t[a][:, m * HK + k, :, :].rearrange("p n r -> p (n r)"),
                                      x1[b][:, k, :], k == 0 and n == 0, k == HK - 1 and n == 2)
                    last.then_inc(z_done, 1)

            mix_group(0)
            pe.wait_ge(a_ready, len(A_PARTS) * RB)
            z_gate_up(0)

            def gate_up(g, i):
                if i >= 2:
                    pe.wait_ge(h_done, Q * g + i - 1)
                pe.wait_ge(w_ready, 2 * (i // QC) + 2)
                at = slice(i * P, (i + 1) * P)
                for m, ps in enumerate((ps_gate, ps_up)):
                    for k in range(HK):
                        for n, (a, b) in enumerate(PASSES):
                            mm(ps[i % 2][:, :], w_gu[m][a][:, k, at], x1[b][:, k, :],
                               k == 0 and n == 0, False)
                    if i == 0:
                        pe.wait_ge(z_ready, 2 * g + m + 1)
                        pe.wait_ge(b_ready, m + 1)
                    bt = slice(m * I + i * P, m * I + (i + 1) * P)
                    for n, (a, b) in enumerate(PASSES):
                        last = mm(ps[i % 2][:, :], b_all[a][:, bt], z[m][b][:, :], False, n == 2)
                last.then_inc(gate_up_done, 1)

            def group(g, more):
                for i in range(Q):
                    gate_up(g, i)
                pe.wait_ge(ident_r_ready, 1)
                for j in range(GT):
                    for k in range(HK):
                        at = slice((j % 2) * H + k * P, (j % 2) * H + (k + 1) * P)
                        for s in (HI, LO):
                            last = mm(ps_out[j // 2][:, at], x1[s][:, k, j * P:(j + 1) * P], ident_r[:, :],
                                      j % 2 == 0 and k == 0 and s == HI, False)
                if more:
                    mix_group(g + 1)
                pe.wait_ge(h_done, Q * g + Q - 1)
                for i in range(Q):
                    pe.wait_ge(h_ready, Q * g + i + 1)
                    for n, (a, b) in enumerate(PASSES):
                        last = mm(ps_gate[0][:, :],
                                  a_t[a][:, 2 * HK + i, :, :].rearrange("p n r -> p (n r)"),
                                  h[b][:, i, :], i == 0 and n == 0, i == Q - 1 and n == 2)
                last.then_inc(zd_done, 1)
                if more:
                    z_gate_up(g + 1)
                pe.wait_ge(wd_ready, 1)
                for j in range(GT):
                    o = ps_out[j // 2][:, (j % 2) * H:(j % 2 + 1) * H]
                    tok = slice(j * P, (j + 1) * P)
                    for i in range(Q):
                        for a, b in PASSES:
                            mm(o, h[a][:, i, tok], wd[b][:, i, :], False, False)
                    if j == 0:
                        pe.wait_ge(zd_ready, g + 1)
                        pe.wait_ge(b_ready, 3)
                    for n, (a, b) in enumerate(PASSES):
                        last = mm(o, zd[a][:, tok], b_all[b][:, 2 * I:], False, j % 2 == 1 and n == 2)
                    if j % 2 == 1:
                        last.then_inc(out_done, 1)

            with pe.Fori(0, GROUPS - 1) as g:
                group(g, True)
            group(GROUPS - 1, False)


_INS = ["x", "itok_B_1_198", "itok_B_0_7", "L0_cond_weights", "L1_cond_Wg", "L1_cond_Wu", "L1_cond_Wd",
        "L1_cond_Ag", "L1_cond_Bg", "L1_cond_Au", "L1_cond_Bu", "L1_cond_Ad", "L1_cond_Bd"]


def kernel(**inputs):
    import numpy as _np
    import concourse.bacc as _bacc
    from concourse import mybir as _mybir
    from concourse.bass_utils import run_bass_kernel_spmd as _run

    nc = _bacc.Bacc("TRN2", target_bir_lowering=False, num_devices=1)
    arrays, args = {}, []
    for name in _INS:
        a = _np.ascontiguousarray(inputs[name])
        arrays[f"in_{name}_dram"] = a
        args.append(nc.dram_tensor(f"in_{name}_dram", a.shape, _mybir.dt.from_np(a.dtype),
                                   kind="ExternalInput").ap())
    out = nc.dram_tensor("out_dram", inputs["x"].shape, _mybir.dt.float32, kind="ExternalOutput").ap()
    cond_lora_block(nc, *args, out)
    r = _run(nc, [arrays], core_ids=[0])
    return r.results[0]["out_dram"]
```

```python
from contextlib import ExitStack

import concourse.bass as bass
from concourse import mybir
from concourse.alu_op_type import AluOpType as ALU

F32 = mybir.dt.float32
F32R = mybir.dt.float32r
I32 = mybir.dt.int32
U32 = mybir.dt.uint32
ACT = mybir.ActivationFunctionType

HI, LO = 0, 1
PASSES = ((HI, HI), (HI, LO), (LO, HI))


def cond_lora_block(
    nc: bass.Bass,
    x: bass.AP,
    condition: bass.AP,
    adapter: bass.AP,
    w_cond: bass.AP,
    Wg: bass.AP,
    Wu: bass.AP,
    Wd: bass.AP,
    Ag: bass.AP,
    Bg: bass.AP,
    Au: bass.AP,
    Bu: bass.AP,
    Ad: bass.AP,
    Bd: bass.AP,
    out: bass.AP,
):
    B, C, H = x.shape
    S = w_cond.shape[0]
    I = Wg.shape[1]
    N, _, R = Ag.shape
    P = 128
    TB = P // C
    TILES = B * C // P
    GT = 4
    T = GT * P
    GROUPS = TILES // GT
    GB = GT * TB
    HK = H // P
    Q = I // P
    WCH = 4
    WC = I // WCH
    QC = Q // WCH
    NR = N * R
    assert NR == P and T == 512 and TB * C == P and H == 256
    AC = 2 * HK + Q
    D_ROWS, K_ROWS = N * Q, N * HK
    WDP = Q // 4
    AW = TB * R
    WAW = AW + H + AW

    tiles_of = lambda ap: ap.rearrange("b c t -> (b c) t").rearrange("(j p) t -> p j t", p=P)
    x_dram = tiles_of(x)
    out_dram = tiles_of(out)
    w_rows = w_cond.rearrange("s c d -> (s c) d")

    with ExitStack() as ctx:
        def sb(name, shape, dt):
            return ctx.enter_context(nc.sbuf_tensor(name, shape, dt))

        def sem(name):
            return ctx.enter_context(nc.semaphore(name))

        ident = sb("ident", [P, P], F32)
        eye_c = sb("eye_c", [P, C], F32)
        p_index = sb("p_index", [P, 1], F32)
        c_index = sb("c_index", [P, 1], F32)
        cond_bc = sb("cond_bc", [P, B], I32)
        adapter_bc = sb("adapter_bc", [P, B], I32)
        w_row_index = sb("w_row_index", [P, TILES], U32)
        mask_d = sb("mask_d", [P, B], F32)
        mask_ge = sb("mask_ge", [P, B], F32)
        half_index = sb("half_index", [P, 1], F32)
        minus_half = sb("minus_half", [P, 1], F32)
        r_index = sb("r_index", [P, 1], F32)
        bd_row_index = sb("bd_row_index", [P, TILES], U32)
        mask = sb("mask", [P, B], F32)
        x_raw = sb("x_raw", [P, GT, H], F32)
        w_gathered = sb("w_gathered", [P, TILES, C], F32)
        mix = sb("mix", [P, GT, P], F32)
        x1 = [sb(f"x1_{s}", [P, HK, T], F32R) for s in ("hi", "lo")]
        x1_whole = sb("x1_whole", [P, HK, T], F32)
        x1_rows = sb("x1_rows", [P, GT, H], F32)
        staged = sb("staged", [P, 2 * HK * I + 2 * I], F32)
        w_gu = [[sb(f"w_{m}_{s}", [P, HK, I], F32R) for s in ("hi", "lo")] for m in ("g", "u")]
        wd_a = [sb(f"wd_a_{s}", [P, Q, WAW], F32R) for s in ("hi", "lo")]
        a_rows = sb("a_rows", [D_ROWS + 2 * K_ROWS, P, R], F32)
        a_t = [sb(f"a_t_{s}", [P, AC, N, R], F32R) for s in ("hi", "lo")]
        b_all = [sb(f"b_{s}", [P, 2 * I], F32R) for s in ("hi", "lo")]
        bd = [sb(f"bd_{s}", [P, GT, H], F32R) for s in ("hi", "lo")]
        z32 = sb("z32", [P, 2, T], F32)
        table_warm = sb("table_warm", [P, 1], F32)
        z = [[sb(f"z_{m}_{s}", [P, T], F32R) for s in ("hi", "lo")] for m in ("g", "u")]
        zd_twice = sb("zd_twice", [P, TB, 2, R], F32)
        zd_turned = sb("zd_turned", [P, P], F32)
        zd_hi = sb("zd_hi", [P, P], F32R)
        zd = [sb(f"zd_{e}", [P, P], F32R) for e in ("even", "odd")]
        h32 = sb("h32", [P, 2, T], F32)
        h = [sb(f"h_{s}", [P, Q, T], F32R) for s in ("hi", "lo")]
        out_sb = sb("out_sb", [P, GT, H], F32)

        bank = [ctx.enter_context(nc.psum_tensor(f"bank{i}", [P, 512], F32)) for i in range(8)]
        ps_gate, ps_up, ps_out, ps_misc = bank[0:2], bank[2:4], bank[4:6], bank[6:8]

        w_raw = [staged[:, m * HK * I:(m + 1) * HK * I].rearrange("p (k n) -> p k n", k=HK) for m in range(2)]
        b_raw = staged[:, 2 * HK * I:]
        wd_raw = staged[:, :HK * I].rearrange("p (q n) -> p q n", q=Q)
        bd_raw = staged[:, HK * I:].rearrange("p (j n) -> p j n", j=TILES)
        wd = [w[:, :, AW:AW + H] for w in wd_a]

        cond_in = sem("cond_in")
        adapter_in = sem("adapter_in")
        x_in = sem("x_in")
        a_gu_in = sem("a_gu_in")
        a_d_in = sem("a_d_in")
        w_in = [sem(f"w_in{c}") for c in range(WCH)]
        b_in = [sem(f"b_in_{m}") for m in ("g", "u")]
        wd_in = sem("wd_in")
        first_gathered = [sem(f"first_gathered{j}") for j in range(GT)]
        gathered = [sem(f"gathered{g}") for g in range(1, GROUPS)]
        consts_ready = sem("consts_ready")
        index_const_ready = sem("index_const_ready")
        ident_memset = sem("ident_memset")
        index_ready = sem("index_ready")
        eye_ready = sem("eye_ready")
        mix_zeroed = sem("mix_zeroed")
        warm_zeroed = sem("warm_zeroed")
        mask_step = sem("mask_step")
        mask_ready = sem("mask_ready")
        mix_ready = sem("mix_ready")
        a_gu_turned = sem("a_gu_turned")
        a_gu_hi_ready = sem("a_gu_hi_ready")
        a_gu_ready = sem("a_gu_ready")
        a_d_turned = sem("a_d_turned")
        a_d_hi_ready = sem("a_d_hi_ready")
        a_d_ready = sem("a_d_ready")
        w_hi_ready = sem("w_hi_ready")
        first_w_ready = sem("first_w_ready")
        w_ready = sem("w_ready")
        b_hi_ready = sem("b_hi_ready")
        b_ready = [sem(f"b_ready_{m}") for m in ("g", "u")]
        r_index_step = sem("r_index_step")
        bd_index_ready = sem("bd_index_ready")
        bd_gathered = [sem(f"bd_gathered{g}") for g in range(GROUPS)]
        bd_hi_ready = sem("bd_hi_ready")
        bd_ready = sem("bd_ready")
        a_gathered = sem("a_gathered")
        wd_hi_ready = sem("wd_hi_ready")
        wd_ready = sem("wd_ready")
        mixed = sem("mixed")
        x1_hi_ready = sem("x1_hi_ready")
        x1_ready = sem("x1_ready")
        z_done = sem("z_done")
        z_masked = sem("z_masked")
        z_hi_ready = sem("z_hi_ready")
        z_ready = [sem(f"z_ready_{m}") for m in ("g", "u")]
        gate_up_done = sem("gate_up_done")
        silu_done = sem("silu_done")
        h_done = sem("h_done")
        h_hi_ready = sem("h_hi_ready")
        h_ready = sem("h_ready")
        x1_whole_ready = sem("x1_whole_ready")
        x1_rows_ready = sem("x1_rows_ready")
        down_done = sem("down_done")
        zd_zeroed = sem("zd_zeroed")
        zd_step = sem("zd_step")
        zd_ready = sem("zd_ready")
        out_done = sem("out_done")
        out_copied = sem("out_copied")
        out_stored = [sem(f"out_stored{b}") for b in range(2)]

        BLOCKS = (P // 32) ** 2

        block = ctx.enter_context(nc.Block())

        def group_mask(g):
            return mask[:, bass.ds(g * GB, GB)].unsqueeze(2).to_broadcast([P, GB, C])

        def by_batch(ap):
            return ap.rearrange("p (b c) -> p b c", c=C)

        def a_turned_gu(m):
            v = ps_out[0][:, :].rearrange("p (r m n c) -> p m n c r", m=2, n=N, c=HK)
            return v[:, m]

        def a_place_gu(s, m):
            return a_t[s][:, m * HK:(m + 1) * HK, :, :].rearrange("p c n r -> p n c r")

        def a_turned_d(half):
            return ps_out[1 - half][:, :].rearrange("p (r n c) -> p n c r", n=N, c=Q)

        def a_place_d(s, half):
            v = a_t[s][:, 2 * HK:, :, half * R // 2:(half + 1) * R // 2]
            return v.rearrange("p c n r -> p n c r")

        def b_lo(eng, ops, m):
            at = slice(m * I, (m + 1) * I)
            eng.wait_ge(b_hi_ready, m + 1)
            ops.tensor_tensor(b_all[LO][:, at], b_raw[:, at], b_all[HI][:, at].bitcast(F32),
                              ALU.subtract).then_inc(b_ready[m], 1)

        def z_lo(eng, ops, g, m):
            eng.wait_ge(z_hi_ready, 2 * g + m + 1)
            ops.tensor_tensor(z[m][LO][:, :], z32[:, m, :], z[m][HI][:, :].bitcast(F32),
                              ALU.subtract).then_inc(z_ready[m], 1)

        def out_place(j):
            b = (ps_out[0], ps_out[1], ps_gate[1], ps_up[1])[j]
            at = AW if j % 2 == 0 else 0
            return b, b[:, at:at + H], b[:, 0:AW] if j % 2 == 0 else b[:, H:H + AW]

        @block.sync
        def _(sp):
            sp.dma_start(cond_bc[:, :], condition.partition_broadcast(P)).then_inc(cond_in, 16)
            sp.dma_start(x_raw[:, :, :], x_dram[:, 0:GT, :]).then_inc(x_in, 16)

            def load_a(row, A):
                n_rows = A.shape[0] * A.shape[1] // P
                sp.dma_start(a_rows[row:row + n_rows, :, :],
                             A.rearrange("n t r -> (n t) r").rearrange("(e p) r -> e p r", p=P))\
                  .then_inc(a_d_in if row == 0 else a_gu_in, 16)

            def load_w(c):
                for m, W in enumerate((Wg, Wu)):
                    sp.dma_start(w_raw[m][:, :, c * WC:(c + 1) * WC],
                                 W.rearrange("(k p) n -> p k n", p=P)[:, :, c * WC:(c + 1) * WC]
                                 ).then_inc(w_in[c], 16)

            load_a(D_ROWS, Ag)
            load_a(D_ROWS + K_ROWS, Au)
            load_w(0)
            for j in range(GT):
                sp.wait_ge(first_gathered[j], 16)
            for m, Bm in enumerate((Bg, Bu)):
                sp.dma_start(b_raw[:, m * I:(m + 1) * I],
                             Bm.rearrange("n r i -> (n r) i")).then_inc(b_in[m], 16)
            load_w(1)
            load_a(0, Ad)
            load_w(2)
            load_w(3)
            def load_x(g):
                tile = g * GT
                sp.dma_start(x_raw[:, :, :], x_dram[:, bass.ds(tile, GT), :]).then_inc(x_in, 16)

            sp.wait_ge(mixed, HK)
            load_x(1)
            sp.wait_ge(first_w_ready, 2)
            sp.wait_ge(w_ready, 2 * (WCH - 1))
            sp.dma_start(wd_raw, Wd.rearrange("(q p) n -> p q n", p=P)).then_inc(wd_in, 16)

            def store(g):
                for b in range(2):
                    sp.wait_ge(out_copied, GT * g + 2 * b + 2)
                    sp.dma_start(out_dram[:, bass.ds(g * GT + 2 * b, 2), :],
                                 out_sb[:, 2 * b:2 * b + 2, :]).then_inc(out_stored[b], 16)

            with sp.Fori(2, GROUPS) as ahead:
                store(ahead - 2)
                sp.wait_ge(mixed, HK * ahead)
                for b in range(2):
                    sp.wait_ge(out_stored[b], 16 * ahead - 16)
                load_x(ahead)
            store(GROUPS - 2)
            store(GROUPS - 1)
            for b in range(2):
                sp.wait_ge(out_stored[b], 16 * GROUPS)

        @block.gpsimd
        def _(pool):
            nc.gpsimd.iota(p_index[:, :], [[0, 1]], base=0, channel_multiplier=1,
                           allow_small_or_imprecise_dtypes=True).then_inc(index_const_ready, 1)
            for q in range(TB):
                pool.wait_ge(index_const_ready, q + 1)
                nc.gpsimd.iota(c_index[q * C:(q + 1) * C, :], [[0, 1]], base=0, channel_multiplier=1,
                               allow_small_or_imprecise_dtypes=True).then_inc(index_const_ready, 1)
            pool.wait_ge(index_const_ready, 1 + TB)
            nc.gpsimd.memset(ident[:, :], 0.0).then_inc(ident_memset, 1)
            pool.wait_ge(ident_memset, 1)
            nc.gpsimd.affine_select(out=ident[:, :], in_=ident[:, :], compare_op=ALU.not_equal, fill=1.0,
                                    base=0, pattern=[[-1, P]], channel_multiplier=1
                                    ).then_inc(consts_ready, 1)
            def gather(first, n):
                for j in range(first, first + n):
                    nc.gpsimd.indirect_dma_start(
                        w_gathered[:, j, :], None, w_rows,
                        bass.IndirectOffsetOnAxis(ap=w_row_index[:, j:j + 1], axis=0),
                    ).then_inc(first_gathered[j] if j < GT else gathered[j // GT - 1], 16)

            pool.wait_ge(index_ready, TB)
            gather(0, GT)

            def x1_sum(g):
                pool.wait_ge(x1_ready, HK * g + HK)
                nc.gpsimd.tensor_tensor(x1_whole[:, :, :], x1[HI][:, :, :].bitcast(F32),
                                        x1[LO][:, :, :].bitcast(F32), ALU.add).then_inc(x1_whole_ready, 1)

            def gather_bd(j):
                nc.gpsimd.indirect_dma_start(
                    bd_raw[:, j, :], None, Bd.rearrange("n r i -> (n r) i"),
                    bass.IndirectOffsetOnAxis(ap=bd_row_index[:, j:j + 1], axis=0),
                ).then_inc(bd_gathered[j // GT], 16)

            for m in range(2):
                pool.wait_ge(w_hi_ready, m + 1)
                nc.gpsimd.tensor_tensor(w_gu[m][LO][:, :, :WC], w_raw[m][:, :, :WC],
                                        w_gu[m][HI][:, :, :WC].bitcast(F32), ALU.subtract
                                        ).then_inc(first_w_ready, 1)
            gather(GT, 3)
            b_lo(pool, nc.gpsimd, 0)
            z_lo(pool, nc.gpsimd, 0, 0)
            gather(GT + 3, 2)
            x1_sum(0)
            pool.wait_ge(bd_index_ready, TB)
            pool.wait_ge(b_ready[1], 1)

            def group(g, first=False, last=False):
                for i in range(Q):
                    pool.wait_ge(h_hi_ready, Q * g + i + 1)
                    nc.gpsimd.tensor_tensor(h[LO][:, i, :], h32[:, i % 2, :], h[HI][:, i, :].bitcast(F32),
                                            ALU.subtract).then_inc(h_ready, 1)
                    if first and i < 4:
                        gather(2 * GT + 1 + 2 * i, min(2, TILES - (2 * GT + 1 + 2 * i)))
                    if first and i == 4:
                        pool.wait_ge(w_ready, 2 * (WCH - 1))
                    if first and i >= 4:
                        gather_bd(2 * i - 8)
                        gather_bd(2 * i - 7)
                if first:
                    for j in range(TILES // 2, TILES):
                        gather_bd(j)
                if not last:
                    for m in range(2):
                        z_lo(pool, nc.gpsimd, g + 1, m)
                    pool.wait_ge(x1_rows_ready, BLOCKS * g + BLOCKS)
                    x1_sum(g + 1)

            group(0, first=True)
            with pool.Fori(1, GROUPS - 1) as g:
                group(g)
            group(GROUPS - 1, last=True)

        @block.scalar
        def _(act):
            act.dma_start(adapter_bc[:, :], adapter.partition_broadcast(P)).then_inc(adapter_in, 16)
            act.wait_ge(index_const_ready, 1)
            nc.scalar.activation(table_warm[:, :], p_index[:, :], ACT.Silu)

            def x1_hi(g):
                for k in range(HK):
                    act.wait_ge(mixed, HK * g + k + 1)
                    nc.scalar.copy(x1[HI][:, k, :], ps_misc[k][:, :]).then_inc(x1_hi_ready, 1)

            def z_hi(g):
                for m in range(2):
                    act.wait_ge(z_masked, 2 * g + m + 1)
                    nc.scalar.copy(z[m][HI][:, :], z32[:, m, :]).then_inc(z_hi_ready, 1)

            def w_hi(c):
                act.wait_ge(w_in[c], 32)
                for m in range(2):
                    nc.scalar.copy(w_gu[m][HI][:, :, c * WC:(c + 1) * WC],
                                   w_raw[m][:, :, c * WC:(c + 1) * WC]).then_inc(w_hi_ready, 1)

            def b_hi(m, columns):
                act.wait_ge(b_in[m], 16)
                nc.scalar.copy(b_all[HI][:, columns], b_raw[:, columns]).then_inc(b_hi_ready, 1)

            def wd_hi(c):
                at = slice(c * WDP, (c + 1) * WDP)
                act.wait_ge(wd_in, 16)
                nc.scalar.copy(wd[HI][:, at, :], wd_raw[:, at, :]).then_inc(wd_hi_ready, 1)

            def adapters(g, j, qs):
                return [act.value_load(adapter_bc[0:1, bass.ds(g * GB + j * TB + q, 1)],
                                       min_val=0, max_val=N - 1) for q in qs]

            def adapters_a(j, qs, values):
                for q, n in zip(qs, values):
                    at = (0 if j % 2 == 0 else AW + H) + q * R
                    for s in (HI, LO):
                        nc.scalar.copy(wd_a[s][:, :, at:at + R],
                                       a_t[s][:, 2 * HK:, bass.ds(n, 1), :].rearrange("p c n r -> p c (n r)")
                                       ).then_inc(a_gathered, 1)

            w_hi(0)
            act.wait_ge(a_gu_turned, 1)
            for m in range(2):
                nc.scalar.copy(a_place_gu(HI, m), a_turned_gu(m)).then_inc(a_gu_hi_ready, 1)
            x1_hi(0)
            b_hi(0, slice(0, I))
            b_hi(1, slice(I, 2 * I))
            z_hi(0)
            w_hi(1)

            def group(g, first=False, last=False):
                for i in range(Q):
                    act.wait_ge(gate_up_done, Q * g + i + 1)
                    if i >= 2:
                        act.wait_ge(h_ready, Q * g + i - 1)
                    nc.scalar.activation(h32[:, i % 2, :], ps_gate[i % 2][:, :], ACT.Silu
                                         ).then_inc(silu_done, 1)
                    if first and i in (0, 2):
                        w_hi(2 + i // 2)
                    if first and i in (1, 3):
                        half = i // 2
                        act.wait_ge(a_d_turned, half + 1)
                        nc.scalar.copy(a_place_d(HI, half), a_turned_d(half)).then_inc(a_d_hi_ready, 1)
                    if first and i >= 4:
                        wd_hi(i - 4)
                    act.wait_ge(h_done, Q * g + i + 1)
                    nc.scalar.copy(h[HI][:, i, :], h32[:, i % 2, :]).then_inc(h_hi_ready, 1)
                    if i == 3:
                        act.wait_ge(a_d_ready, 2)
                        if not first:
                            act.wait_ge(down_done, GT * g)
                    if 3 <= i < Q - 1:
                        j, qs = (i - 3) // 2, range((i - 3) % 2 * TB // 2, ((i - 3) % 2 + 1) * TB // 2)
                        adapters_a(j, qs, adapters(g, j, qs))
                if not last:
                    x1_hi(g + 1)
                if first:
                    act.wait_ge(bd_gathered[0], 16 * GT)
                else:
                    act.wait_ge(out_done, GT * g)
                nc.scalar.copy(bd[HI][:, :, :], bd_raw[:, bass.ds(g * GT, GT), :]).then_inc(bd_hi_ready, 1)
                for j in (2, 3):
                    values = adapters(g, j, range(TB))
                    act.wait_ge(down_done, GT * g + j - 1)
                    adapters_a(j, range(TB), values)
                if not last:
                    z_hi(g + 1)
                if first:
                    for later in bd_gathered[1:]:
                        act.wait_ge(later, 16 * GT)

            group(0, first=True)
            with act.Fori(1, GROUPS - 1) as g:
                group(g)
            group(GROUPS - 1, last=True)

        @block.vector
        def _(dve):
            nc.vector.memset(z[0][HI][:, :].bitcast(F32), 0.0).then_inc(warm_zeroed, 1)
            nc.vector.memset(mix[:, :, :], 0.0).then_inc(mix_zeroed, 1)
            nc.vector.memset(zd_turned[:, :], 0.0).then_inc(zd_zeroed, 1)
            dve.wait_ge(index_const_ready, 1 + TB)
            dve.wait_ge(cond_in, 16)
            for q in range(TB):
                at = slice(q * C, (q + 1) * C)
                nc.vector.tensor_scalar(w_row_index[at, :], cond_bc[at, q::TB], float(C), c_index[at, :],
                                        ALU.mult, ALU.add).then_inc(index_ready, 1)
            dve.wait_ge(consts_ready, 1)
            for q in range(TB):
                at = slice(q * C, (q + 1) * C)
                nc.vector.tensor_copy(eye_c[at, :], ident[at, at]).then_inc(eye_ready, 1)
            dve.wait_ge(adapter_in, 16)
            nc.vector.tensor_scalar(mask_d[:, :], adapter_bc[:, :], -float(R), p_index[:, :],
                                    ALU.mult, ALU.add).then_inc(mask_step, 1)
            dve.wait_ge(mask_step, 1)
            nc.vector.tensor_scalar(mask_ge[:, :], mask_d[:, :], 0.0, None, ALU.is_ge).then_inc(mask_step, 1)
            dve.wait_ge(mask_step, 2)
            nc.vector.scalar_tensor_tensor(mask[:, :], mask_d[:, :], R - 0.5, mask_ge[:, :],
                                           ALU.is_lt, ALU.mult).then_inc(mask_ready, 1)

            nc.vector.tensor_scalar(half_index[:, :], c_index[:, :], R - 0.5, None, ALU.is_gt
                                    ).then_inc(r_index_step, 1)
            dve.wait_ge(r_index_step, 1)
            nc.vector.tensor_scalar(minus_half[:, :], half_index[:, :], -1.0, None, ALU.mult
                                    ).then_inc(r_index_step, 1)
            nc.vector.scalar_tensor_tensor(r_index[:, :], half_index[:, :], -float(R), c_index[:, :],
                                           ALU.mult, ALU.add).then_inc(r_index_step, 1)
            dve.wait_ge(r_index_step, 3)
            for q in range(TB):
                at = slice(q * C, (q + 1) * C)
                nc.vector.tensor_scalar(bd_row_index[at, :], adapter_bc[at, q::TB], float(R), r_index[at, :],
                                        ALU.mult, ALU.add).then_inc(bd_index_ready, 1)

            def mix_tiles(g, tiles):
                for q in range(TB):
                    at = slice(q * C, (q + 1) * C)
                    n = tiles.stop - tiles.start
                    nc.vector.tensor_tensor(mix[at, tiles, at],
                                            w_gathered[at, bass.ds(g * GT + tiles.start, n), :],
                                            eye_c[at, :].unsqueeze(1).to_broadcast([C, n, C]),
                                            ALU.add).then_inc(mix_ready, 1)

            def x1_lo(g):
                for k in range(HK):
                    dve.wait_ge(x1_hi_ready, HK * g + k + 1)
                    nc.vector.tensor_tensor(x1[LO][:, k, :], ps_misc[k][:, :], x1[HI][:, k, :].bitcast(F32),
                                            ALU.subtract).then_inc(x1_ready, 1)

            def z_mask(g):
                for m in range(2):
                    dve.wait_ge(z_done, 2 * g + m + 1)
                    nc.vector.tensor_tensor(by_batch(z32[:, m, :]), by_batch(ps_misc[m][:, :]),
                                            group_mask(g), ALU.mult).then_inc(z_masked, 1)

            def w_lo(c):
                for m in range(2):
                    dve.wait_ge(w_hi_ready, 2 * c + m + 1)
                    nc.vector.tensor_tensor(w_gu[m][LO][:, :, c * WC:(c + 1) * WC],
                                            w_raw[m][:, :, c * WC:(c + 1) * WC],
                                            w_gu[m][HI][:, :, c * WC:(c + 1) * WC].bitcast(F32),
                                            ALU.subtract).then_inc(w_ready, 1)

            def wd_lo(c):
                at = slice(c * WDP, (c + 1) * WDP)
                dve.wait_ge(wd_hi_ready, c + 1)
                nc.vector.tensor_tensor(wd[LO][:, at, :], wd_raw[:, at, :], wd[HI][:, at, :].bitcast(F32),
                                        ALU.subtract).then_inc(wd_ready, 1)

            dve.wait_ge(mix_zeroed, 1)
            dve.wait_ge(eye_ready, TB)
            for j in range(GT):
                dve.wait_ge(first_gathered[j], 16)
                mix_tiles(0, slice(j, j + 1))
            dve.wait_ge(a_gu_hi_ready, 2)
            for m in range(2):
                nc.vector.tensor_tensor(a_place_gu(LO, m), a_turned_gu(m), a_place_gu(HI, m).bitcast(F32),
                                        ALU.subtract).then_inc(a_gu_ready, 1)
            x1_lo(0)
            b_lo(dve, nc.vector, 1)
            dve.wait_ge(mask_ready, 1)
            z_mask(0)
            z_lo(dve, nc.vector, 0, 1)
            w_lo(1)

            def turn_x1(n):
                a, b = n // (P // 32), n % (P // 32)
                src = x1_whole[32 * a:32 * a + 32, :, :].rearrange("p k (j b t) -> p k j b t", b=P // 32, t=32)
                dst = x1_rows[32 * b:32 * b + 32, :, :].rearrange("p j (k a t) -> p k j a t", k=HK, t=32)
                nc.vector.transpose(dst[:, :, :, a, :].bitcast(U32), src[:, :, :, b, :].bitcast(U32)
                                    ).then_inc(x1_rows_ready, 1)

            def zd_parts(g, j):
                steps = (TB + 2) * (GT * g + j)
                dve.wait_ge(down_done, GT * g + j + 1)
                nc.vector.tensor_copy(zd_twice[:, :, :, :],
                                      out_place(j)[2].rearrange("p (q r) -> p q r", q=TB).unsqueeze(2)
                                      .to_broadcast([P, TB, 2, R])).then_inc(zd_step, 1)
                dve.wait_ge(zd_step, steps + 1)
                for q in range(TB):
                    at = slice(q * C, (q + 1) * C)
                    nc.vector.transpose(zd_turned[at, at].bitcast(U32),
                                        zd_twice[at, q, :, :].rearrange("p h r -> p (h r)").bitcast(U32)
                                        ).then_inc(zd_step, 1)
                dve.wait_ge(zd_step, steps + 1 + TB)
                nc.vector.tensor_copy(zd_hi[:, :], zd_turned[:, :]).then_inc(zd_step, 1)
                dve.wait_ge(zd_step, steps + 2 + TB)
                nc.vector.scalar_tensor_tensor(zd[j % 2][:, :], zd_hi[:, :].bitcast(F32), minus_half[:, :],
                                               zd_turned[:, :], ALU.mult, ALU.add).then_inc(zd_ready, 1)

            def copy_out(g, j, last):
                dve.wait_ge(out_done, GT * g + j + 1)
                if last and j % 2 == 0:
                    dve.wait_ge(out_stored[j // 2], 16 * g)
                nc.vector.tensor_tensor(out_sb[:, j, :], out_place(j)[1], x1_rows[:, j, :],
                                        ALU.add).then_inc(out_copied, 1)

            def group(g, first=False, last=False):
                for i in range(Q):
                    dve.wait_ge(silu_done, Q * g + i + 1)
                    nc.vector.tensor_tensor(h32[:, i % 2, :], h32[:, i % 2, :], ps_up[i % 2][:, :],
                                            ALU.mult).then_inc(h_done, 1)
                    if first and i in (0, 2):
                        w_lo(2 + i // 2)
                    if first and i in (1, 3):
                        half = i // 2
                        dve.wait_ge(a_d_hi_ready, half + 1)
                        nc.vector.tensor_tensor(a_place_d(LO, half), a_turned_d(half),
                                                a_place_d(HI, half).bitcast(F32),
                                                ALU.subtract).then_inc(a_d_ready, 1)
                    if first and i >= 4:
                        wd_lo(i - 4)
                    if i == 2:
                        dve.wait_ge(x1_whole_ready, g + 1)
                    if i >= 2:
                        for n in range(BLOCKS * (i - 2) // (Q - 2), BLOCKS * (i - 1) // (Q - 2)):
                            turn_x1(n)
                    if not last and i == 5:
                        dve.wait_ge(mixed, HK * g + HK)
                        if first:
                            dve.wait_ge(gathered[0], 16 * GT)
                        mix_tiles(g + 1, slice(0, GT))
                if first:
                    for later in gathered[1:]:
                        dve.wait_ge(later, 16 * GT)
                if not last:
                    x1_lo(g + 1)
                dve.wait_ge(bd_hi_ready, g + 1)
                nc.vector.tensor_tensor(bd[LO][:, :, :], bd_raw[:, bass.ds(g * GT, GT), :],
                                        bd[HI][:, :, :].bitcast(F32), ALU.subtract).then_inc(bd_ready, 1)
                dve.wait_ge(x1_rows_ready, BLOCKS * g + BLOCKS)
                for j in range(GT):
                    zd_parts(g, j)
                    if j >= 1:
                        copy_out(g, j - 1, last)
                if not last:
                    z_mask(g + 1)
                copy_out(g, GT - 1, last)

            group(0, first=True)
            with dve.Fori(1, GROUPS - 1) as g:
                group(g)
            group(GROUPS - 1, last=True)

        @block.tensor
        def _(pe):
            def turn_a(rows, o, ranks):
                width = rows.stop - rows.start
                for e, r in enumerate(ranks):
                    last = nc.tensor.transpose(o[:, e * width:(e + 1) * width], a_rows[rows, :, r],
                                               ident[rows, rows])
                return last

            def warm_up(n):
                for _ in range(n):
                    nc.tensor.matmul(ps_gate[1][:, :], z[0][HI][:, :P], z[0][HI][:, :], start=True, stop=True,
                                     skip_group_check=True)

            pe.wait_ge(warm_zeroed, 1)
            warm_up(10)
            pe.wait_ge(consts_ready, 1)
            pe.wait_ge(a_gu_in, 32)
            turn_a(slice(D_ROWS, D_ROWS + 2 * K_ROWS), ps_out[0], range(R)).then_inc(a_gu_turned, 1)

            def turn_a_d(half):
                turn_a(slice(0, D_ROWS), ps_out[1 - half], range(half * R // 2, (half + 1) * R // 2)
                       ).then_inc(a_d_turned, 1)

            def mm(o, lhsT, rhs, start, stop):
                return nc.tensor.matmul(o, lhsT, rhs, start=start, stop=stop, skip_group_check=True)

            def x1_part(j, k):
                return mm(ps_misc[k][:, j * P:(j + 1) * P], x_raw[:, j, k * P:(k + 1) * P], mix[:, j, :],
                          j == 0, j == GT - 1)

            def mix_group(g):
                pe.wait_ge(x_in, 16 * g + 16)
                pe.wait_ge(mix_ready, GT * TB + TB * g)
                for k in range(HK):
                    for j in range(GT):
                        last = x1_part(j, k)
                    last.then_inc(mixed, 1)

            def z_gate_up(g):
                pe.wait_ge(x1_ready, HK * g + HK)
                for m in range(2):
                    for k in range(HK):
                        for n, (a, b) in enumerate(PASSES):
                            last = mm(ps_misc[m][:, :],
                                      a_t[a][:, m * HK + k, :, :].rearrange("p n r -> p (n r)"),
                                      x1[b][:, k, :], k == 0 and n == 0, k == HK - 1 and n == 2)
                    last.then_inc(z_done, 1)

            def gate_up_base(g, i):
                if i >= 2:
                    pe.wait_ge(h_done, Q * g + i - 1)
                if i >= QC:
                    pe.wait_ge(w_ready, 2 * (i // QC))
                for m, ps in enumerate((ps_gate, ps_up)):
                    for k in range(HK):
                        for n, (a, b) in enumerate(PASSES):
                            mm(ps[i % 2][:, :], w_gu[m][a][:, k, i * P:(i + 1) * P], x1[b][:, k, :],
                               k == 0 and n == 0, False)

            def gate_up_lora(g, i):
                for m, ps in enumerate((ps_gate, ps_up)):
                    if i == 0:
                        pe.wait_ge(z_ready[m], g + 1)
                        pe.wait_ge(b_ready[m], 1)
                    at = slice(m * I + i * P, m * I + (i + 1) * P)
                    for n, (a, b) in enumerate(PASSES):
                        last = mm(ps[i % 2][:, :], b_all[a][:, at], z[m][b][:, :], False, n == 2)
                last.then_inc(gate_up_done, 1)

            warm_up(8)
            pe.wait_ge(x_in, 16)
            for j in range(GT):
                pe.wait_ge(mix_ready, TB * (j + 1))
                for k in range(HK):
                    last = x1_part(j, k)
                    if j == GT - 1:
                        last.then_inc(mixed, 1)
            for b in (HI, LO):
                for k in range(HK):
                    pe.wait_ge(x1_ready if b == LO else x1_hi_ready, k + 1)
                    for m, ps in enumerate((ps_gate, ps_up)):
                        if b == HI and k == 0:
                            pe.wait_ge(first_w_ready, m + 1)
                        for a in ((HI, LO) if b == HI else (HI,)):
                            mm(ps[0][:, :], w_gu[m][a][:, k, 0:P], x1[b][:, k, :],
                               a == HI and b == HI and k == 0, False)
            pe.wait_ge(a_gu_ready, 2)
            z_gate_up(0)
            gate_up_base(0, 1)
            pe.wait_ge(a_d_in, 16)
            for half in range(2):
                turn_a_d(half)

            def group(g, first=False, last=False):
                for i in range(Q):
                    if i == 1 and not first:
                        pe.wait_ge(out_copied, GT * g)
                    if not (first and i < 2):
                        gate_up_base(g, i)
                    gate_up_lora(g, i)
                if not last:
                    mix_group(g + 1)
                if first:
                    pe.wait_ge(wd_ready, Q // WDP)

                def down(j):
                    b = out_place(j)[0][:, 0:H + AW]
                    beside = slice(0, AW + H) if j % 2 == 0 else slice(AW, WAW)
                    pe.wait_ge(a_gathered, 2 * TB * GT * g + 2 * TB * (j + 1))
                    if j == 2:
                        pe.wait_ge(h_done, Q * g + Q)
                    for i in range(Q):
                        if j == 0:
                            pe.wait_ge(h_ready, Q * g + i + 1)
                        for n, (a, c) in enumerate(PASSES):
                            done = mm(b, h[a][:, i, j * P:(j + 1) * P], wd_a[c][:, i, beside],
                                      i == 0 and n == 0, False)
                    done.then_inc(down_done, 1)

                def down_lora(j):
                    if j == 0:
                        pe.wait_ge(bd_ready, g + 1)
                    pe.wait_ge(zd_ready, GT * g + j + 1)
                    for s in (HI, LO):
                        done = mm(out_place(j)[1], zd[j % 2][:, :], bd[s][:, j, :], False, s == LO)
                    done.then_inc(out_done, 1)

                for j in range(GT):
                    down(j)
                    if j >= 1:
                        down_lora(j - 1)
                if not last:
                    z_gate_up(g + 1)
                down_lora(GT - 1)

            group(0, first=True)
            with pe.Fori(1, GROUPS - 1) as g:
                group(g)
            group(GROUPS - 1, last=True)


_INS = ["x", "itok_B_1_198", "itok_B_0_7", "L0_cond_weights", "L1_cond_Wg", "L1_cond_Wu", "L1_cond_Wd",
        "L1_cond_Ag", "L1_cond_Bg", "L1_cond_Au", "L1_cond_Bu", "L1_cond_Ad", "L1_cond_Bd"]


def kernel(**inputs):
    import numpy as _np
    import concourse.bacc as _bacc
    from concourse import mybir as _mybir
    from concourse.bass_utils import run_bass_kernel_spmd as _run

    nc = _bacc.Bacc("TRN2", target_bir_lowering=False, num_devices=1)
    arrays, args = {}, []
    for name in _INS:
        a = _np.ascontiguousarray(inputs[name])
        arrays[f"in_{name}_dram"] = a
        args.append(nc.dram_tensor(f"in_{name}_dram", a.shape, _mybir.dt.from_np(a.dtype),
                                   kind="ExternalInput").ap())
    out = nc.dram_tensor("out_dram", inputs["x"].shape, _mybir.dt.float32, kind="ExternalOutput").ap()
    cond_lora_block(nc, *args, out)
    r = _run(nc, [arrays], core_ids=[0])
    return r.results[0]["out_dram"]
```

```python
from contextlib import ExitStack

import concourse.bass as bass
from concourse import mybir
from concourse.alu_op_type import AluOpType as ALU

F32 = mybir.dt.float32
F32R = mybir.dt.float32r
I32 = mybir.dt.int32
U32 = mybir.dt.uint32
ACT = mybir.ActivationFunctionType

HI, LO = 0, 1
PASSES = ((HI, HI), (HI, LO), (LO, HI))


def cond_lora_block(
    nc: bass.Bass,
    x: bass.AP,
    condition: bass.AP,
    adapter: bass.AP,
    w_cond: bass.AP,
    Wg: bass.AP,
    Wu: bass.AP,
    Wd: bass.AP,
    Ag: bass.AP,
    Bg: bass.AP,
    Au: bass.AP,
    Bu: bass.AP,
    Ad: bass.AP,
    Bd: bass.AP,
    out: bass.AP,
):
    B, C, H = x.shape
    I = Wg.shape[1]
    N, _, R = Ag.shape
    P = 128
    TB = P // C
    TILES = B * C // P
    GT = 4
    T = GT * P
    GROUPS = TILES // GT
    GB = GT * TB
    HK = H // P
    Q = I // P
    WCH = 4
    WC = I // WCH
    QC = Q // WCH
    NR = N * R
    assert NR == P and T == 512 and TB * C == P and H == 256
    AC = 2 * HK + Q
    D_ROWS, K_ROWS = N * Q, N * HK
    WDP = Q // 4
    AW = TB * R
    WAW = AW + H + AW

    tiles_of = lambda ap: ap.rearrange("b c t -> (b c) t").rearrange("(j p) t -> p j t", p=P)
    x_dram = tiles_of(x)
    out_dram = tiles_of(out)
    w_rows = w_cond.rearrange("s c d -> (s c) d")

    with ExitStack() as ctx:
        def sb(name, shape, dt):
            return ctx.enter_context(nc.sbuf_tensor(name, shape, dt))

        def sem(name):
            return ctx.enter_context(nc.semaphore(name))

        ident = sb("ident", [P, P], F32)
        eye_c = sb("eye_c", [P, C], F32)
        p_index = sb("p_index", [P, 1], F32)
        c_index = sb("c_index", [P, 1], F32)
        cond_bc = sb("cond_bc", [P, B], I32)
        adapter_bc = sb("adapter_bc", [P, B], I32)
        w_row_index = sb("w_row_index", [P, TILES], U32)
        mask_d = sb("mask_d", [P, B], F32)
        mask_ge = sb("mask_ge", [P, B], F32)
        half_index = sb("half_index", [P, 1], F32)
        minus_half = sb("minus_half", [P, 1], F32)
        r_index = sb("r_index", [P, 1], F32)
        bd_row_index = sb("bd_row_index", [P, TILES], U32)
        mask = sb("mask", [P, B], F32)
        x_raw = sb("x_raw", [P, GT, H], F32)
        w_gathered = sb("w_gathered", [P, TILES, C], F32)
        mix = sb("mix", [P, GT, P], F32)
        x1 = [sb(f"x1_{s}", [P, HK, T], F32R) for s in ("hi", "lo")]
        x1_whole = sb("x1_whole", [P, HK, T], F32)
        x1_rows = sb("x1_rows", [P, GT, H], F32)
        staged = sb("staged", [P, 2 * HK * I + 2 * I], F32)
        w_gu = [[sb(f"w_{m}_{s}", [P, HK, I], F32R) for s in ("hi", "lo")] for m in ("g", "u")]
        wd_a = [sb(f"wd_a_{s}", [P, Q, WAW], F32R) for s in ("hi", "lo")]
        a_rows = sb("a_rows", [D_ROWS + 2 * K_ROWS, P, R], F32)
        a_t = [sb(f"a_t_{s}", [P, AC, N, R], F32R) for s in ("hi", "lo")]
        b_all = [sb(f"b_{s}", [P, 2 * I], F32R) for s in ("hi", "lo")]
        bd = [sb(f"bd_{s}", [P, GT, H], F32R) for s in ("hi", "lo")]
        z32 = sb("z32", [P, 2, T], F32)
        table_warm = sb("table_warm", [P, 1], F32)
        z = [[sb(f"z_{m}_{s}", [P, T], F32R) for s in ("hi", "lo")] for m in ("g", "u")]
        own_row = sb("own_row", [P, TB, 2, R], F32)
        zd_twice = sb("zd_twice", [P, TB, 2, R], F32)
        zd_turned = sb("zd_turned", [P, P], F32)
        zd_hi = sb("zd_hi", [P, P], F32R)
        zd = [sb(f"zd_{e}", [P, P], F32R) for e in ("even", "odd")]
        h32 = sb("h32", [P, 2, T], F32)
        h = [sb(f"h_{s}", [P, Q, T], F32R) for s in ("hi", "lo")]
        out_sb = sb("out_sb", [P, GT, H], F32)

        bank = [ctx.enter_context(nc.psum_tensor(f"bank{i}", [P, 512], F32)) for i in range(8)]
        ps_gate, ps_up, ps_out, ps_misc = bank[0:2], bank[2:4], bank[4:6], bank[6:8]

        w_raw = [staged[:, m * HK * I:(m + 1) * HK * I].rearrange("p (k n) -> p k n", k=HK) for m in range(2)]
        b_raw = staged[:, 2 * HK * I:]
        wd_raw = staged[:, :HK * I].rearrange("p (q n) -> p q n", q=Q)
        bd_raw = staged[:, HK * I:].rearrange("p (j n) -> p j n", j=TILES)
        wd = [w[:, :, AW:AW + H] for w in wd_a]

        cond_in = sem("cond_in")
        adapter_in = sem("adapter_in")
        x_in = sem("x_in")
        a_gu_in = sem("a_gu_in")
        a_d_in = sem("a_d_in")
        w_in = [sem(f"w_in{c}") for c in range(WCH)]
        b_in = [sem(f"b_in_{m}") for m in ("g", "u")]
        wd_in = sem("wd_in")
        first_gathered = [sem(f"first_gathered{j}") for j in range(GT)]
        gathered = [sem(f"gathered{g}") for g in range(1, GROUPS)]
        consts_ready = sem("consts_ready")
        index_const_ready = sem("index_const_ready")
        ident_memset = sem("ident_memset")
        index_ready = sem("index_ready")
        eye_ready = sem("eye_ready")
        mix_zeroed = sem("mix_zeroed")
        warm_zeroed = sem("warm_zeroed")
        mask_step = sem("mask_step")
        mask_ready = sem("mask_ready")
        mix_ready = sem("mix_ready")
        a_gu_turned = sem("a_gu_turned")
        a_gu_hi_ready = sem("a_gu_hi_ready")
        a_gu_ready = sem("a_gu_ready")
        a_d_turned = sem("a_d_turned")
        a_d_hi_ready = sem("a_d_hi_ready")
        a_d_ready = sem("a_d_ready")
        w_hi_ready = sem("w_hi_ready")
        first_w_ready = sem("first_w_ready")
        w_ready = sem("w_ready")
        b_hi_ready = sem("b_hi_ready")
        b_ready = [sem(f"b_ready_{m}") for m in ("g", "u")]
        r_index_step = sem("r_index_step")
        bd_index_ready = sem("bd_index_ready")
        bd_gathered = [sem(f"bd_gathered{g}") for g in range(GROUPS)]
        bd_hi_ready = sem("bd_hi_ready")
        bd_ready = sem("bd_ready")
        a_gathered = sem("a_gathered")
        wd_hi_ready = sem("wd_hi_ready")
        wd_ready = sem("wd_ready")
        mixed = sem("mixed")
        x1_hi_ready = sem("x1_hi_ready")
        x1_ready = sem("x1_ready")
        early_mixed = sem("early_mixed")
        early_x1_hi_ready = sem("early_x1_hi_ready")
        early_x1_ready = sem("early_x1_ready")
        z_done = sem("z_done")
        z_masked = sem("z_masked")
        z_hi_ready = sem("z_hi_ready")
        z_ready = [sem(f"z_ready_{m}") for m in ("g", "u")]
        gate_up_done = sem("gate_up_done")
        silu_done = sem("silu_done")
        h_done = sem("h_done")
        h_hi_ready = sem("h_hi_ready")
        h_ready = sem("h_ready")
        x1_whole_ready = sem("x1_whole_ready")
        x1_rows_ready = sem("x1_rows_ready")
        down_done = sem("down_done")
        own_row_ready = sem("own_row_ready")
        zd_step = sem("zd_step")
        zd_ready = sem("zd_ready")
        out_done = sem("out_done")
        out_copied = sem("out_copied")
        out_stored = [sem(f"out_stored{b}") for b in range(2)]

        BLOCKS = (P // 32) ** 2

        block = ctx.enter_context(nc.Block())

        def group_mask(g):
            return mask[:, bass.ds(g * GB, GB)].unsqueeze(2).to_broadcast([P, GB, C])

        def by_batch(ap):
            return ap.rearrange("p (b c) -> p b c", c=C)

        def a_turned_gu(m):
            v = ps_out[0][:, :].rearrange("p (r m n c) -> p m n c r", m=2, n=N, c=HK)
            return v[:, m]

        def a_place_gu(s, m):
            return a_t[s][:, m * HK:(m + 1) * HK, :, :].rearrange("p c n r -> p n c r")

        def a_turned_d(half):
            return ps_out[1 - half][:, :].rearrange("p (r n c) -> p n c r", n=N, c=Q)

        def a_place_d(s, half):
            v = a_t[s][:, 2 * HK:, :, half * R // 2:(half + 1) * R // 2]
            return v.rearrange("p c n r -> p n c r")

        def b_lo(eng, ops, m):
            at = slice(m * I, (m + 1) * I)
            eng.wait_ge(b_hi_ready, m + 1)
            ops.tensor_tensor(b_all[LO][:, at], b_raw[:, at], b_all[HI][:, at].bitcast(F32),
                              ALU.subtract).then_inc(b_ready[m], 1)

        def z_lo(eng, ops, g, m):
            eng.wait_ge(z_hi_ready, 2 * g + m + 1)
            ops.tensor_tensor(z[m][LO][:, :], z32[:, m, :], z[m][HI][:, :].bitcast(F32),
                              ALU.subtract).then_inc(z_ready[m], 1)

        halves = (slice(0, T // 2), slice(T // 2, T))
        half_banks = (ps_misc, (ps_out[1], ps_out[0]))

        def out_place(j):
            b = (ps_out[0], ps_out[1], ps_gate[1], ps_up[1])[j]
            at = AW if j % 2 == 0 else 0
            return b, b[:, at:at + H], b[:, 0:AW] if j % 2 == 0 else b[:, H:H + AW]

        @block.sync
        def _(sp):
            sp.dma_start(cond_bc[:, :], condition.partition_broadcast(P)).then_inc(cond_in, 16)
            sp.dma_start(x_raw[:, :, :], x_dram[:, 0:GT, :]).then_inc(x_in, 16)

            def load_a(row, A):
                n_rows = A.shape[0] * A.shape[1] // P
                sp.dma_start(a_rows[row:row + n_rows, :, :],
                             A.rearrange("n t r -> (n t) r").rearrange("(e p) r -> e p r", p=P))\
                  .then_inc(a_d_in if row == 0 else a_gu_in, 16)

            def load_w(c):
                for m, W in enumerate((Wg, Wu)):
                    sp.dma_start(w_raw[m][:, :, c * WC:(c + 1) * WC],
                                 W.rearrange("(k p) n -> p k n", p=P)[:, :, c * WC:(c + 1) * WC]
                                 ).then_inc(w_in[c], 16)

            load_a(D_ROWS, Ag)
            load_a(D_ROWS + K_ROWS, Au)
            load_w(0)
            for j in range(GT):
                sp.wait_ge(first_gathered[j], 16)
            for m, Bm in enumerate((Bg, Bu)):
                sp.dma_start(b_raw[:, m * I:(m + 1) * I],
                             Bm.rearrange("n r i -> (n r) i")).then_inc(b_in[m], 16)
            load_w(1)
            load_a(0, Ad)
            load_w(2)
            load_w(3)
            def load_x(g):
                tile = g * GT
                sp.dma_start(x_raw[:, :, :], x_dram[:, bass.ds(tile, GT), :]).then_inc(x_in, 16)

            sp.wait_ge(mixed, HK)
            load_x(1)
            sp.wait_ge(first_w_ready, 2)
            sp.wait_ge(w_ready, 2 * (WCH - 1))
            sp.dma_start(wd_raw, Wd.rearrange("(q p) n -> p q n", p=P)).then_inc(wd_in, 16)

            def store(g):
                for b in range(2):
                    sp.wait_ge(out_copied, GT * g + 2 * b + 2)
                    sp.dma_start(out_dram[:, bass.ds(g * GT + 2 * b, 2), :],
                                 out_sb[:, 2 * b:2 * b + 2, :]).then_inc(out_stored[b], 16)

            with sp.Fori(2, GROUPS) as ahead:
                store(ahead - 2)
                sp.wait_ge(mixed, HK * ahead)
                for b in range(2):
                    sp.wait_ge(out_stored[b], 16 * ahead - 16)
                load_x(ahead)
            store(GROUPS - 2)
            for j in range(GT):
                sp.wait_ge(out_copied, GT * (GROUPS - 1) + j + 1)
                sp.dma_start(out_dram[:, (GROUPS - 1) * GT + j, :], out_sb[:, j, :]
                             ).then_inc(out_stored[j // 2], 16)
            for b in range(2):
                sp.wait_ge(out_stored[b], 16 * (GROUPS + 1))

        @block.gpsimd
        def _(pool):
            nc.gpsimd.iota(p_index[:, :], [[0, 1]], base=0, channel_multiplier=1,
                           allow_small_or_imprecise_dtypes=True).then_inc(index_const_ready, 1)
            for q in range(TB):
                pool.wait_ge(index_const_ready, q + 1)
                nc.gpsimd.iota(c_index[q * C:(q + 1) * C, :], [[0, 1]], base=0, channel_multiplier=1,
                               allow_small_or_imprecise_dtypes=True).then_inc(index_const_ready, 1)
            pool.wait_ge(index_const_ready, 1 + TB)
            nc.gpsimd.memset(ident[:, :], 0.0).then_inc(ident_memset, 1)
            pool.wait_ge(ident_memset, 1)
            nc.gpsimd.affine_select(out=ident[:, :], in_=ident[:, :], compare_op=ALU.not_equal, fill=1.0,
                                    base=0, pattern=[[-1, P]], channel_multiplier=1
                                    ).then_inc(consts_ready, 1)
            def gather(first, n):
                for j in range(first, first + n):
                    nc.gpsimd.indirect_dma_start(
                        w_gathered[:, j, :], None, w_rows,
                        bass.IndirectOffsetOnAxis(ap=w_row_index[:, j:j + 1], axis=0),
                    ).then_inc(first_gathered[j] if j < GT else gathered[j // GT - 1], 16)

            pool.wait_ge(index_ready, TB)
            gather(0, GT)

            def x1_sum(g):
                pool.wait_ge(x1_ready, HK * g + HK)
                nc.gpsimd.tensor_tensor(x1_whole[:, :, :], x1[HI][:, :, :].bitcast(F32),
                                        x1[LO][:, :, :].bitcast(F32), ALU.add).then_inc(x1_whole_ready, 1)

            def gather_bd(j):
                nc.gpsimd.indirect_dma_start(
                    bd_raw[:, j, :], None, Bd.rearrange("n r i -> (n r) i"),
                    bass.IndirectOffsetOnAxis(ap=bd_row_index[:, j:j + 1], axis=0),
                ).then_inc(bd_gathered[j // GT], 16)

            for m in range(2):
                pool.wait_ge(w_hi_ready, m + 1)
                nc.gpsimd.tensor_tensor(w_gu[m][LO][:, :, :WC], w_raw[m][:, :, :WC],
                                        w_gu[m][HI][:, :, :WC].bitcast(F32), ALU.subtract
                                        ).then_inc(first_w_ready, 1)
            gather(GT, 3)
            b_lo(pool, nc.gpsimd, 0)
            z_lo(pool, nc.gpsimd, 0, 0)
            gather(GT + 3, 2)
            x1_sum(0)
            pool.wait_ge(bd_index_ready, TB)
            pool.wait_ge(b_ready[1], 1)

            def group(g, first=False, last=False):
                for i in range(Q):
                    pool.wait_ge(h_hi_ready, Q * g + i + 1)
                    nc.gpsimd.tensor_tensor(h[LO][:, i, :], h32[:, i % 2, :], h[HI][:, i, :].bitcast(F32),
                                            ALU.subtract).then_inc(h_ready, 1)
                    if first and i < 4:
                        gather(2 * GT + 1 + 2 * i, min(2, TILES - (2 * GT + 1 + 2 * i)))
                    if first and i == 4:
                        pool.wait_ge(w_ready, 2 * (WCH - 1))
                    if first and i >= 4:
                        gather_bd(2 * i - 8)
                        gather_bd(2 * i - 7)
                if first:
                    for j in range(TILES // 2, TILES):
                        gather_bd(j)
                if not last:
                    for m in range(2):
                        z_lo(pool, nc.gpsimd, g + 1, m)
                    pool.wait_ge(x1_rows_ready, BLOCKS * g + BLOCKS)
                    x1_sum(g + 1)

            group(0, first=True)
            with pool.Fori(1, GROUPS - 1) as g:
                group(g)
            group(GROUPS - 1, last=True)

        @block.scalar
        def _(act):
            act.dma_start(adapter_bc[:, :], adapter.partition_broadcast(P)).then_inc(adapter_in, 16)
            act.wait_ge(index_const_ready, 1)
            nc.scalar.activation(table_warm[:, :], p_index[:, :], ACT.Silu)

            def x1_hi(g):
                for k in range(HK):
                    act.wait_ge(mixed, HK * g + k + 1)
                    nc.scalar.copy(x1[HI][:, k, :], ps_misc[k][:, :]).then_inc(x1_hi_ready, 1)

            def first_x1_hi(e):
                for k in range(HK):
                    act.wait_ge((early_mixed, mixed)[e], k + 1)
                    nc.scalar.copy(x1[HI][:, k, halves[e]], half_banks[e][k][:, halves[e]]
                                   ).then_inc((early_x1_hi_ready, x1_hi_ready)[e], 1)

            def z_hi(g):
                for m in range(2):
                    act.wait_ge(z_masked, 2 * g + m + 1)
                    nc.scalar.copy(z[m][HI][:, :], z32[:, m, :]).then_inc(z_hi_ready, 1)

            def w_hi(c):
                act.wait_ge(w_in[c], 32)
                for m in range(2):
                    nc.scalar.copy(w_gu[m][HI][:, :, c * WC:(c + 1) * WC],
                                   w_raw[m][:, :, c * WC:(c + 1) * WC]).then_inc(w_hi_ready, 1)

            def b_hi(m, columns):
                act.wait_ge(b_in[m], 16)
                nc.scalar.copy(b_all[HI][:, columns], b_raw[:, columns]).then_inc(b_hi_ready, 1)

            def wd_hi(c):
                at = slice(c * WDP, (c + 1) * WDP)
                act.wait_ge(wd_in, 16)
                nc.scalar.copy(wd[HI][:, at, :], wd_raw[:, at, :]).then_inc(wd_hi_ready, 1)

            def bd_hi(g):
                nc.scalar.copy(bd[HI][:, :, :], bd_raw[:, bass.ds(g * GT, GT), :]).then_inc(bd_hi_ready, 1)

            def adapters(g, j):
                row = adapter_bc[0:1, bass.ds(g * GB + j * TB, TB)]
                return nc.values_load_multi_w_load_instructions(
                    row, engines=(mybir.EngineType.Activation,), min_val=0, max_val=N - 1)[1]

            def adapters_a(j, values):
                for q, n in enumerate(values):
                    at = (0 if j % 2 == 0 else AW + H) + q * R
                    for s in (HI, LO):
                        nc.scalar.copy(wd_a[s][:, :, at:at + R],
                                       a_t[s][:, 2 * HK:, bass.ds(n, 1), :].rearrange("p c n r -> p c (n r)")
                                       ).then_inc(a_gathered, 1)

            w_hi(0)
            act.wait_ge(a_gu_turned, 1)
            for m in range(2):
                nc.scalar.copy(a_place_gu(HI, m), a_turned_gu(m)).then_inc(a_gu_hi_ready, 1)
            for e in range(2):
                first_x1_hi(e)
            b_hi(0, slice(0, I))
            b_hi(1, slice(I, 2 * I))
            z_hi(0)
            w_hi(1)

            def group(g, first=False, last=False):
                for i in range(Q):
                    act.wait_ge(gate_up_done, Q * g + i + 1)
                    if i >= 2:
                        act.wait_ge(h_ready, Q * g + i - 1)
                    nc.scalar.activation(h32[:, i % 2, :], ps_gate[i % 2][:, :], ACT.Silu
                                         ).then_inc(silu_done, 1)
                    if first and i in (0, 2):
                        w_hi(2 + i // 2)
                    if first and i in (1, 3):
                        half = i // 2
                        act.wait_ge(a_d_turned, half + 1)
                        nc.scalar.copy(a_place_d(HI, half), a_turned_d(half)).then_inc(a_d_hi_ready, 1)
                    if first and i >= 4:
                        wd_hi(i - 4)
                    act.wait_ge(h_done, Q * g + i + 1)
                    nc.scalar.copy(h[HI][:, i, :], h32[:, i % 2, :]).then_inc(h_hi_ready, 1)
                    if i == 2 and not first:
                        act.wait_ge(out_done, GT * g)
                        bd_hi(g)
                    if i == 3:
                        if first:
                            act.wait_ge(adapter_in, 16)
                        act.wait_ge(a_d_ready, 2)
                        if not first:
                            act.wait_ge(down_done, GT * g)
                    if i in (3, 5):
                        j = (i - 3) // 2
                        adapters_a(j, adapters(g, j))
                if not last:
                    x1_hi(g + 1)
                if first:
                    act.wait_ge(bd_gathered[0], 16 * GT)
                    bd_hi(g)
                values = [adapters(g, j) for j in (2, 3)]
                for j in (2, 3):
                    act.wait_ge(down_done, GT * g + j - 1)
                    adapters_a(j, values[j - 2])
                if not last:
                    z_hi(g + 1)
                if first:
                    for later in bd_gathered[1:]:
                        act.wait_ge(later, 16 * GT)

            group(0, first=True)
            with act.Fori(1, GROUPS - 1) as g:
                group(g)
            group(GROUPS - 1, last=True)

        @block.vector
        def _(dve):
            nc.vector.memset(z[0][HI][:, :].bitcast(F32), 0.0).then_inc(warm_zeroed, 1)
            nc.vector.memset(mix[:, :, :], 0.0).then_inc(mix_zeroed, 1)
            nc.vector.memset(own_row[:, :, :, :], 0.0).then_inc(own_row_ready, 1)
            dve.wait_ge(index_const_ready, 1 + TB)
            dve.wait_ge(cond_in, 16)
            for q in range(TB):
                at = slice(q * C, (q + 1) * C)
                nc.vector.tensor_scalar(w_row_index[at, :], cond_bc[at, q::TB], float(C), c_index[at, :],
                                        ALU.mult, ALU.add).then_inc(index_ready, 1)
            dve.wait_ge(consts_ready, 1)
            for q in range(TB):
                at = slice(q * C, (q + 1) * C)
                nc.vector.tensor_copy(eye_c[at, :], ident[at, at]).then_inc(eye_ready, 1)
            dve.wait_ge(adapter_in, 16)
            nc.vector.tensor_scalar(mask_d[:, :], adapter_bc[:, :], -float(R), p_index[:, :],
                                    ALU.mult, ALU.add).then_inc(mask_step, 1)
            dve.wait_ge(mask_step, 1)
            nc.vector.tensor_scalar(mask_ge[:, :], mask_d[:, :], 0.0, None, ALU.is_ge).then_inc(mask_step, 1)
            dve.wait_ge(mask_step, 2)
            nc.vector.scalar_tensor_tensor(mask[:, :], mask_d[:, :], R - 0.5, mask_ge[:, :],
                                           ALU.is_lt, ALU.mult).then_inc(mask_ready, 1)

            dve.wait_ge(own_row_ready, 1)
            for q in range(TB):
                nc.vector.memset(own_row[q * C:(q + 1) * C, q, :, :], 1.0).then_inc(own_row_ready, 1)
            nc.vector.tensor_scalar(half_index[:, :], c_index[:, :], R - 0.5, None, ALU.is_gt
                                    ).then_inc(r_index_step, 1)
            dve.wait_ge(r_index_step, 1)
            nc.vector.tensor_scalar(minus_half[:, :], half_index[:, :], -1.0, None, ALU.mult
                                    ).then_inc(r_index_step, 1)
            nc.vector.scalar_tensor_tensor(r_index[:, :], half_index[:, :], -float(R), c_index[:, :],
                                           ALU.mult, ALU.add).then_inc(r_index_step, 1)
            dve.wait_ge(r_index_step, 3)
            for q in range(TB):
                at = slice(q * C, (q + 1) * C)
                nc.vector.tensor_scalar(bd_row_index[at, :], adapter_bc[at, q::TB], float(R), r_index[at, :],
                                        ALU.mult, ALU.add).then_inc(bd_index_ready, 1)

            def mix_tiles(g, tiles):
                for q in range(TB):
                    at = slice(q * C, (q + 1) * C)
                    n = tiles.stop - tiles.start
                    nc.vector.tensor_tensor(mix[at, tiles, at],
                                            w_gathered[at, bass.ds(g * GT + tiles.start, n), :],
                                            eye_c[at, :].unsqueeze(1).to_broadcast([C, n, C]),
                                            ALU.add).then_inc(mix_ready, 1)

            def x1_lo(g):
                for k in range(HK):
                    dve.wait_ge(x1_hi_ready, HK * g + k + 1)
                    nc.vector.tensor_tensor(x1[LO][:, k, :], ps_misc[k][:, :], x1[HI][:, k, :].bitcast(F32),
                                            ALU.subtract).then_inc(x1_ready, 1)

            def z_mask(g, ms=range(2)):
                for m in ms:
                    dve.wait_ge(z_done, 2 * g + m + 1)
                    nc.vector.tensor_tensor(by_batch(z32[:, m, :]), by_batch(ps_misc[m][:, :]),
                                            group_mask(g), ALU.mult).then_inc(z_masked, 1)

            def w_lo(c):
                for m in range(2):
                    dve.wait_ge(w_hi_ready, 2 * c + m + 1)
                    nc.vector.tensor_tensor(w_gu[m][LO][:, :, c * WC:(c + 1) * WC],
                                            w_raw[m][:, :, c * WC:(c + 1) * WC],
                                            w_gu[m][HI][:, :, c * WC:(c + 1) * WC].bitcast(F32),
                                            ALU.subtract).then_inc(w_ready, 1)

            def wd_lo(c):
                at = slice(c * WDP, (c + 1) * WDP)
                dve.wait_ge(wd_hi_ready, c + 1)
                nc.vector.tensor_tensor(wd[LO][:, at, :], wd_raw[:, at, :], wd[HI][:, at, :].bitcast(F32),
                                        ALU.subtract).then_inc(wd_ready, 1)

            dve.wait_ge(mix_zeroed, 1)
            dve.wait_ge(eye_ready, TB)
            for j in range(GT):
                if j == GT - 1:
                    dve.wait_ge(a_gu_hi_ready, 2)
                    for m in range(2):
                        nc.vector.tensor_tensor(a_place_gu(LO, m), a_turned_gu(m),
                                                a_place_gu(HI, m).bitcast(F32),
                                                ALU.subtract).then_inc(a_gu_ready, 1)
                dve.wait_ge(first_gathered[j], 16)
                mix_tiles(0, slice(j, j + 1))
            for e in range(2):
                for k in range(HK):
                    dve.wait_ge((early_x1_hi_ready, x1_hi_ready)[e], k + 1)
                    nc.vector.tensor_tensor(x1[LO][:, k, halves[e]], half_banks[e][k][:, halves[e]],
                                            x1[HI][:, k, halves[e]].bitcast(F32),
                                            ALU.subtract).then_inc((early_x1_ready, x1_ready)[e], 1)
            dve.wait_ge(mask_ready, 1)
            z_mask(0, (0,))
            b_lo(dve, nc.vector, 1)
            z_mask(0, (1,))
            z_lo(dve, nc.vector, 0, 1)
            w_lo(1)

            def turn_x1(n):
                a, b = n // (P // 32), n % (P // 32)
                src = x1_whole[32 * a:32 * a + 32, :, :].rearrange("p k (j b t) -> p k j b t", b=P // 32, t=32)
                dst = x1_rows[32 * b:32 * b + 32, :, :].rearrange("p j (k a t) -> p k j a t", k=HK, t=32)
                nc.vector.transpose(dst[:, :, :, a, :].bitcast(U32), src[:, :, :, b, :].bitcast(U32)
                                    ).then_inc(x1_rows_ready, 1)

            def bd_lo(g):
                dve.wait_ge(bd_hi_ready, g + 1)
                nc.vector.tensor_tensor(bd[LO][:, :, :], bd_raw[:, bass.ds(g * GT, GT), :],
                                        bd[HI][:, :, :].bitcast(F32), ALU.subtract).then_inc(bd_ready, 1)

            def zd_parts(g, j):
                steps = 3 * (GT * g + j)
                dve.wait_ge(down_done, GT * g + j + 1)
                nc.vector.tensor_tensor(zd_twice[:, :, :, :],
                                        out_place(j)[2].rearrange("p (q r) -> p q r", q=TB).unsqueeze(2)
                                        .to_broadcast([P, TB, 2, R]), own_row[:, :, :, :],
                                        ALU.mult).then_inc(zd_step, 1)
                dve.wait_ge(zd_step, steps + 1)
                nc.vector.transpose(zd_turned[:, :].bitcast(U32),
                                    zd_twice[:, :, :, :].rearrange("p q h r -> p (q h r)").bitcast(U32)
                                    ).then_inc(zd_step, 1)
                dve.wait_ge(zd_step, steps + 2)
                nc.vector.tensor_copy(zd_hi[:, :], zd_turned[:, :]).then_inc(zd_step, 1)
                dve.wait_ge(zd_step, steps + 3)
                nc.vector.scalar_tensor_tensor(zd[j % 2][:, :], zd_hi[:, :].bitcast(F32), minus_half[:, :],
                                               zd_turned[:, :], ALU.mult, ALU.add).then_inc(zd_ready, 1)

            def copy_out(g, j, last):
                dve.wait_ge(out_done, GT * g + j + 1)
                if last and j % 2 == 0:
                    dve.wait_ge(out_stored[j // 2], 16 * g)
                nc.vector.tensor_tensor(out_sb[:, j, :], out_place(j)[1], x1_rows[:, j, :],
                                        ALU.add).then_inc(out_copied, 1)

            def group(g, first=False, last=False):
                if first:
                    dve.wait_ge(own_row_ready, 1 + TB)
                for i in range(Q):
                    dve.wait_ge(silu_done, Q * g + i + 1)
                    nc.vector.tensor_tensor(h32[:, i % 2, :], h32[:, i % 2, :], ps_up[i % 2][:, :],
                                            ALU.mult).then_inc(h_done, 1)
                    if first and i in (0, 2):
                        w_lo(2 + i // 2)
                    if first and i in (1, 3):
                        half = i // 2
                        dve.wait_ge(a_d_hi_ready, half + 1)
                        nc.vector.tensor_tensor(a_place_d(LO, half), a_turned_d(half),
                                                a_place_d(HI, half).bitcast(F32),
                                                ALU.subtract).then_inc(a_d_ready, 1)
                    if first and i >= 4:
                        wd_lo(i - 4)
                    if i == 2:
                        dve.wait_ge(x1_whole_ready, g + 1)
                    if i >= 2:
                        for n in range(BLOCKS * (i - 2) // (Q - 2), BLOCKS * (i - 1) // (Q - 2)):
                            turn_x1(n)
                    if i == 3 and not first:
                        bd_lo(g)
                    if not last and i == 5:
                        dve.wait_ge(mixed, HK * g + HK)
                        if first:
                            dve.wait_ge(gathered[0], 16 * GT)
                        mix_tiles(g + 1, slice(0, GT))
                if first:
                    for later in gathered[1:]:
                        dve.wait_ge(later, 16 * GT)
                if not last:
                    x1_lo(g + 1)
                if first:
                    bd_lo(g)
                dve.wait_ge(x1_rows_ready, BLOCKS * g + BLOCKS)
                for j in range(GT):
                    zd_parts(g, j)
                    if j >= 1:
                        copy_out(g, j - 1, last)
                if not last:
                    z_mask(g + 1)
                copy_out(g, GT - 1, last)

            group(0, first=True)
            with dve.Fori(1, GROUPS - 1) as g:
                group(g)
            group(GROUPS - 1, last=True)

        @block.tensor
        def _(pe):
            def turn_a(rows, o, ranks):
                width = rows.stop - rows.start
                for e, r in enumerate(ranks):
                    last = nc.tensor.transpose(o[:, e * width:(e + 1) * width], a_rows[rows, :, r],
                                               ident[rows, rows])
                return last

            def warm_up(n):
                for _ in range(n):
                    nc.tensor.matmul(ps_gate[1][:, :], z[0][HI][:, :P], z[0][HI][:, :], start=True, stop=True,
                                     skip_group_check=True)

            pe.wait_ge(warm_zeroed, 1)
            warm_up(10)
            pe.wait_ge(consts_ready, 1)
            pe.wait_ge(a_gu_in, 32)
            turn_a(slice(D_ROWS, D_ROWS + 2 * K_ROWS), ps_out[0], range(R)).then_inc(a_gu_turned, 1)

            def turn_a_d(half):
                turn_a(slice(0, D_ROWS), ps_out[1 - half], range(half * R // 2, (half + 1) * R // 2)
                       ).then_inc(a_d_turned, 1)

            def mm(o, lhsT, rhs, start, stop):
                return nc.tensor.matmul(o, lhsT, rhs, start=start, stop=stop, skip_group_check=True)

            def x1_part(banks, j, k, first, last):
                return mm(banks[k][:, j * P:(j + 1) * P], x_raw[:, j, k * P:(k + 1) * P], mix[:, j, :],
                          j == first, j == last)

            def mix_group(g):
                pe.wait_ge(x_in, 16 * g + 16)
                pe.wait_ge(mix_ready, GT * TB + TB * g)
                for k in range(HK):
                    for j in range(GT):
                        last = x1_part(ps_misc, j, k, 0, GT - 1)
                    last.then_inc(mixed, 1)

            def z_gate_up(g):
                pe.wait_ge(x1_ready, HK * g + HK)
                for m in range(2):
                    for k in range(HK):
                        for n, (a, b) in enumerate(PASSES):
                            last = mm(ps_misc[m][:, :],
                                      a_t[a][:, m * HK + k, :, :].rearrange("p n r -> p (n r)"),
                                      x1[b][:, k, :], k == 0 and n == 0, k == HK - 1 and n == 2)
                    last.then_inc(z_done, 1)

            def gate_up_base(g, i):
                if i >= 2:
                    pe.wait_ge(h_done, Q * g + i - 1)
                if i >= QC:
                    pe.wait_ge(w_ready, 2 * (i // QC))
                for m, ps in enumerate((ps_gate, ps_up)):
                    for k in range(HK):
                        for n, (a, b) in enumerate(PASSES):
                            mm(ps[i % 2][:, :], w_gu[m][a][:, k, i * P:(i + 1) * P], x1[b][:, k, :],
                               k == 0 and n == 0, False)

            def gate_up_lora(g, i):
                for m, ps in enumerate((ps_gate, ps_up)):
                    if i == 0:
                        pe.wait_ge(z_ready[m], g + 1)
                        pe.wait_ge(b_ready[m], 1)
                    at = slice(m * I + i * P, m * I + (i + 1) * P)
                    for n, (a, b) in enumerate(PASSES):
                        last = mm(ps[i % 2][:, :], b_all[a][:, at], z[m][b][:, :], False, n == 2)
                last.then_inc(gate_up_done, 1)

            warm_up(5)
            def first_x1(j):
                e = j // (GT // 2)
                first = e * (GT // 2)
                pe.wait_ge(mix_ready, TB * (j + 1))
                for k in range(HK):
                    last = x1_part(half_banks[e], j, k, first, first + GT // 2 - 1)
                    if j == first + GT // 2 - 1:
                        last.then_inc((early_mixed, mixed)[e], 1)

            def first_base(e, a, b):
                for k in range(HK):
                    if a == HI:
                        hi, lo = ((early_x1_hi_ready, early_x1_ready), (x1_hi_ready, x1_ready))[e]
                        pe.wait_ge(lo if b == LO else hi, k + 1)
                    for m, ps in enumerate((ps_gate, ps_up)):
                        if a == LO and k == 0:
                            pe.wait_ge(first_w_ready, m + 1)
                        mm(ps[0][:, halves[e]], w_gu[m][a][:, k, 0:P], x1[b][:, k, halves[e]],
                           e == 0 and a == HI and b == HI and k == 0, False)

            pe.wait_ge(x_in, 16)
            first_x1(0)
            first_x1(1)
            pe.wait_ge(w_hi_ready, 2)
            first_base(0, HI, HI)
            pe.wait_ge(a_gu_ready, 2)
            first_x1(2)
            first_x1(3)
            first_base(0, LO, HI)
            first_base(0, HI, LO)
            for a, b in ((HI, HI), (LO, HI), (HI, LO)):
                first_base(1, a, b)
            z_gate_up(0)
            gate_up_base(0, 1)

            def group(g, first=False, last=False):
                for i in range(Q):
                    if i == 1 and not first:
                        pe.wait_ge(out_copied, GT * g)
                    if not (first and i < 2):
                        gate_up_base(g, i)
                    gate_up_lora(g, i)
                    if first and i == 0:
                        pe.wait_ge(a_d_in, 16)
                        for half in range(2):
                            turn_a_d(half)
                if not last:
                    mix_group(g + 1)
                def down(j, parts=range(Q)):
                    b = out_place(j)[0][:, 0:H + AW]
                    beside = slice(0, AW + H) if j % 2 == 0 else slice(AW, WAW)
                    pe.wait_ge(a_gathered, 2 * TB * GT * g + 2 * TB * (j + 1))
                    if j == 2:
                        pe.wait_ge(h_done, Q * g + Q)
                    for i in parts:
                        if j == 0:
                            pe.wait_ge(h_ready, Q * g + i + 1)
                        if j == 0 and first:
                            pe.wait_ge(wd_ready, i // WDP + 1)
                        for n, (a, c) in enumerate(PASSES):
                            done = mm(b, h[a][:, i, j * P:(j + 1) * P], wd_a[c][:, i, beside],
                                      i == 0 and n == 0, False)
                    if Q - 1 in parts:
                        done.then_inc(down_done, 1)

                def down_lora(j):
                    if j == 0:
                        pe.wait_ge(bd_ready, g + 1)
                    pe.wait_ge(zd_ready, GT * g + j + 1)
                    for s in (HI, LO):
                        done = mm(out_place(j)[1], zd[j % 2][:, :], bd[s][:, j, :], False, s == LO)
                    done.then_inc(out_done, 1)

                if last:
                    down(0, range(Q - 1))
                    down(1, range(Q // 2))
                    down(0, range(Q - 1, Q))
                    down(1, range(Q // 2, Q))
                for j in range(GT):
                    if not (last and j < 2):
                        down(j)
                    if j >= 1:
                        down_lora(j - 1)
                if not last:
                    z_gate_up(g + 1)
                down_lora(GT - 1)

            group(0, first=True)
            with pe.Fori(1, GROUPS - 1) as g:
                group(g)
            group(GROUPS - 1, last=True)


_INS = ["x", "itok_B_1_198", "itok_B_0_7", "L0_cond_weights", "L1_cond_Wg", "L1_cond_Wu", "L1_cond_Wd",
        "L1_cond_Ag", "L1_cond_Bg", "L1_cond_Au", "L1_cond_Bu", "L1_cond_Ad", "L1_cond_Bd"]


def kernel(**inputs):
    import numpy as _np
    import concourse.bacc as _bacc
    from concourse import mybir as _mybir
    from concourse.bass_utils import run_bass_kernel_spmd as _run

    nc = _bacc.Bacc("TRN2", target_bir_lowering=False, num_devices=1)
    arrays, args = {}, []
    for name in _INS:
        a = _np.ascontiguousarray(inputs[name])
        arrays[f"in_{name}_dram"] = a
        args.append(nc.dram_tensor(f"in_{name}_dram", a.shape, _mybir.dt.from_np(a.dtype),
                                   kind="ExternalInput").ap())
    out = nc.dram_tensor("out_dram", inputs["x"].shape, _mybir.dt.float32, kind="ExternalOutput").ap()
    cond_lora_block(nc, *args, out)
    r = _run(nc, [arrays], core_ids=[0])
    return r.results[0]["out_dram"]
```
